# Optimizing a Trainium2 kernel written in Bass

```python
import numpy as np
import jax
import jax.numpy as jnp

def _softmax(x, axis=-1):
    return jax.nn.softmax(x, axis=axis)

def _gelu(x):
    return jax.nn.gelu(x, approximate=True)

def _silu(x):
    return jax.nn.silu(x)

def _sigmoid(x):
    return jax.nn.sigmoid(x)

def _layernorm(x, axis=-1, eps=1e-05):
    m = jnp.mean(x, axis=axis, keepdims=True)
    v = jnp.var(x, axis=axis, keepdims=True)
    return (x - m) / jnp.sqrt(v + eps)

def _scatter_add(tgt, idx, src, axis=0):
    return tgt.at[idx].add(src)

def _segment_sum(src, seg, n):
    return jax.ops.segment_sum(src, seg, n)
kernel_name = 'mk_adj_resnorm_d2_adj_r2_dfec11'

def setup_inputs(seed: int=0):
    np.random.seed(seed)
    _w = jnp.asarray

    def _rec_inputs():
        import jax
        import jax.numpy as jnp
        _gk = jax.random.key(seed)
        x = -0.000929 + 1 * jax.random.normal(jax.random.fold_in(_gk, 1), (4096, 128), jnp.float32)
        _a = jax.random.bernoulli(jax.random.fold_in(_gk, 2), 0.000976562, (4096, 4096))
        _a = jnp.logical_or(_a, jnp.swapaxes(_a, -1, -2))
        _a = jnp.logical_or(_a, jnp.eye(4096, dtype=bool))
        adj = _a.astype(jnp.int32)
        return (x, adj)
    x, adj = _rec_inputs()

    def _L0_gnn_setup():
        import jax, jax.numpy as jnp
        import numpy as np
        NEG_INF = -9000000000000000.0
        ALPHA = 0.2
        key = jax.random.key(seed)
        k1, k2, k3, k4 = jax.random.split(key, 4)
        N, F_IN, H, D = (4096, 128, 4, 32)
        h = jax.random.normal(k1, (N, F_IN), dtype=jnp.float32)
        adj = jax.random.randint(k2, (N, N), 0, 2, dtype=jnp.int32)
        W = jax.random.normal(k3, (F_IN, H * D), dtype=jnp.float32) * (1.0 / np.sqrt(F_IN))
        a = jax.random.normal(k4, (1, H, 2 * D), dtype=jnp.float32)
        return {'h': h, 'adj': adj, 'W': W, 'a': a}
    _L0_gnn_all = _L0_gnn_setup()
    _L0_gnn_in = {k: v for k, v in _L0_gnn_all.items() if k in ('W', 'a')}
    del _L0_gnn_all

    def _L1_gnn_setup():
        import jax, jax.numpy as jnp
        import numpy as np
        EPS = 1e-07
        MAX_NORM = 1.0 - 0.001
        ALPHA = 0.2
        NEG_INF = -9000000000000000.0

        def _proj(x, max_norm=MAX_NORM):
            norm = jnp.clip(jnp.linalg.norm(x, axis=-1, keepdims=True), EPS)
            return jnp.where(norm > max_norm, x / norm * max_norm, x)

        def _logmap0(x):
            norm = jnp.clip(jnp.linalg.norm(x, axis=-1, keepdims=True), EPS, 1.0 - EPS)
            return jnp.arctanh(norm) * x / norm

        def _expmap0(v):
            norm = jnp.clip(jnp.linalg.norm(v, axis=-1, keepdims=True), EPS)
            return jnp.tanh(norm) * v / norm
        key = jax.random.key(seed)
        k1, k2, k3 = jax.random.split(key, 3)
        N, D = (6144, 128)
        x = jax.random.normal(k1, (N, D), dtype=jnp.float32) * 0.01
        adj = jax.random.randint(k2, (N, N), 0, 2, dtype=jnp.int32)
        a = jax.random.normal(k3, (2 * D, 1), dtype=jnp.float32) * 0.2
        a = _proj(a, 0.9)
        return {'x': x, 'adj': adj, 'a': a}
    _L1_gnn_all = _L1_gnn_setup()
    _L1_gnn_in = {k: v for k, v in _L1_gnn_all.items() if k in ('a',)}
    del _L1_gnn_all
    return {'x': x, 'adj': adj, 'L0_gnn_W': _L0_gnn_in['W'], 'L0_gnn_a': _L0_gnn_in['a'], 'L1_gnn_a': _L1_gnn_in['a']}

def reference(x, adj, L0_gnn_W, L0_gnn_a, L1_gnn_a):
    import jax
    import jax.numpy as jnp

    def _L0_gnn_ref(h, adj, W, a):
        import jax, jax.numpy as jnp
        import numpy as np
        NEG_INF = -9000000000000000.0
        ALPHA = 0.2
        N = h.shape[0]
        H = a.shape[1]
        D = a.shape[2] // 2
        Wh = (h @ W).reshape(N, H, D)
        a_src = a[0, :, :D]
        a_dst = a[0, :, D:]
        s_src = jnp.einsum('nhd,hd->nh', Wh, a_src)
        s_dst = jnp.einsum('nhd,hd->nh', Wh, a_dst)
        e = s_src[:, None, :] + s_dst[None, :, :]
        e = jnp.where(e >= 0, e, ALPHA * e)
        e = jnp.where(adj[:, :, None] > 0, e, NEG_INF)
        attention = jax.nn.softmax(e, axis=1)
        h_prime = jnp.einsum('ijh,jhd->ihd', attention, Wh)
        return jax.nn.elu(h_prime.reshape(N, H * D))

    def _L1_gnn_ref(x, adj, a):
        import jax, jax.numpy as jnp
        import numpy as np
        EPS = 1e-07
        MAX_NORM = 1.0 - 0.001
        ALPHA = 0.2
        NEG_INF = -9000000000000000.0

        def _proj(x, max_norm=MAX_NORM):
            norm = jnp.clip(jnp.linalg.norm(x, axis=-1, keepdims=True), EPS)
            return jnp.where(norm > max_norm, x / norm * max_norm, x)

        def _logmap0(x):
            norm = jnp.clip(jnp.linalg.norm(x, axis=-1, keepdims=True), EPS, 1.0 - EPS)
            return jnp.arctanh(norm) * x / norm

        def _expmap0(v):
            norm = jnp.clip(jnp.linalg.norm(v, axis=-1, keepdims=True), EPS)
            return jnp.tanh(norm) * v / norm
        D = a.shape[0] // 2
        x_tan = _logmap0(x)
        wh1 = x_tan @ a[:D]
        wh2 = x_tan @ a[D:]
        e = jax.nn.leaky_relu(wh1 + wh2.T, ALPHA)
        scores = jnp.where(adj > 0, e, NEG_INF)
        attention = jax.nn.softmax(scores, axis=1)
        x_tan_prime = attention @ x_tan
        return _proj(_expmap0(x_tan_prime))
    x = _layernorm(x + _L0_gnn_ref(x, adj, L0_gnn_W, L0_gnn_a), axis=-1)
    x = _layernorm(x + _L1_gnn_ref(x, adj, L1_gnn_a), axis=-1)
    return x

_drawn_inputs = setup_inputs


def setup_inputs(seed=0):
    import zlib

    import numpy as np

    out = dict(_drawn_inputs(seed))
    spreads = {}
    factors = {}
    for name, (base, spread) in spreads.items():
        noise = np.random.default_rng([zlib.crc32(name.encode()), seed]).standard_normal(out[name].shape)
        drawn = base * np.exp(spread * noise) if base else spread * noise
        out[name] = jnp.asarray(drawn.astype(out[name].dtype))
    for name, factor in factors.items():
        out[name] = (out[name] * factor).astype(out[name].dtype)
    return out
```

```python
import concourse.bass as bass
from concourse import mybir
from contextlib import ExitStack

F32, BF16, I32 = mybir.dt.float32, mybir.dt.bfloat16, mybir.dt.int32
ALU = mybir.AluOpType
ACT = mybir.ActivationFunctionType
AXX = mybir.AxisListType.X

P = 128
SLOPE = 0.2
NEG_INF = 9.0e15
EPS = 1e-7
MAX_NORM = 1.0 - 0.001
LN_EPS = 1e-5
BANK = 512


class Chain:

    def __init__(self, engine, semaphore):
        self.engine, self.semaphore, self.count = engine, semaphore, 0

    def __call__(self, instruction):
        self.count += 1
        instruction.then_inc(self.semaphore, 1)
        self.engine.wait_ge(self.semaphore, self.count)


def two_layer_gat(nc, x, adj, W, a0, a1, out):
    N, F = x.shape
    H, D = a0.shape[1], a0.shape[2] // 2
    T = N // P
    x_rows = x.rearrange("(t p) f -> p t f", p=P)
    out_rows = out.rearrange("(t p) f -> p t f", p=P)

    ctx = ExitStack()
    with ctx:
        def sb(name, shape, dt=F32, where=ctx):
            return where.enter_context(nc.sbuf_tensor(name, shape, dt))

        def pb(name, shape, dt=F32, where=ctx):
            return where.enter_context(nc.psum_tensor(name, shape, dt))

        def sem(name):
            return ctx.enter_context(nc.semaphore(name))

        ident = sb("ident", [P, P])
        feat = sb("feat", [P, T, F])
        featT = sb("featT", [P, N])
        values = sb("values", [P, T, F])
        summed = sb("summed", [P, T, F])
        scores = sb("scores", [P, T, 2 * H])
        proj = sb("proj", [P, F + 2 * H])
        a1_cols = sb("a1_cols", [P, 2])
        spread = sb("spread", [P, H, P])
        banks = [pb(f"bank{i}", [P, BANK]) for i in range(8)]

        a0_row = sb("a0_row", [1, 2 * H * D])
        a1_row = sb("a1_row", [1, 2 * F])
        ones_row = sb("ones_row", [1, P])
        wa = sb("wa", [P, 2, H, D])
        x_in, small_in = sem("x_in"), sem("small_in")
        ident_zero, ident_ready, ones_ready = sem("ident_zero"), sem("ident_ready"), sem("ones_ready")
        a0_spread, a1_turned, dve0 = sem("a0_spread"), sem("a1_turned"), sem("dve0")
        proj_ready, transposed, T_copied = sem("proj_ready"), sem("transposed"), sem("T_copied")
        projected, taken = sem("projected"), sem("taken")

        with nc.Block() as block:
            @block.sync
            def _(sp):
                sp.dma_start(proj[:, 0:F], W).then_inc(small_in, 16)
                sp.dma_start(a0_row[:, :], a0.rearrange("o h e -> o (h e)")).then_inc(small_in, 16)
                sp.dma_start(a1_row[:, :], a1.rearrange("f o -> o f")).then_inc(small_in, 16)
                sp.dma_start(feat[:, :, :], x_rows).then_inc(x_in, 16)

            @block.gpsimd
            def _(pool):
                pool.memset(ones_row[:, :], 1.0).then_inc(ones_ready, 1)
                pool.memset(ident[:, :], 0.0).then_inc(ident_zero, 1)
                pool.wait_ge(ident_zero, 1)
                pool.affine_select(out=ident[:, :], in_=ident[:, :], compare_op=ALU.not_equal, fill=1.0, base=0,
                                   pattern=[[-1, P]], channel_multiplier=1).then_inc(ident_ready, 1)

            @block.tensor
            def _(pe):
                pe.wait_ge(small_in, 48)
                pe.wait_ge(ones_ready, 1)
                pe.matmul(banks[7][:, 0:2 * H * D], ones_row[:, :], a0_row[:, :], start=True, stop=True)\
                    .then_inc(a0_spread, 1)
                for k in range(2):
                    last = pe.matmul(banks[6][:, k:k + 1], a1_row[:, k * F:(k + 1) * F], ones_row[:, 0:1],
                                     start=True, stop=True)
                last.then_inc(a1_turned, 1)
                pe.wait_ge(x_in, 16)
                pe.wait_ge(ident_ready, 1)
                for n in range(T // 4):
                    if n >= 2:
                        pe.wait_ge(T_copied, n - 1)
                    for t in range(4 * n, 4 * n + 4):
                        last = pe.transpose(banks[n % 2][:, (t % 4) * P:(t % 4 + 1) * P], feat[:, t, :], ident[:, :])
                    last.then_inc(transposed, 1)
                pe.wait_ge(T_copied, T // 4)
                pe.wait_ge(proj_ready, 1)
                for t in range(T):
                    if t >= 4:
                        pe.wait_ge(taken, t - 3)
                    pe.matmul(banks[2 + t % 4][:, 0:F + 2 * H], featT[:, t * P:(t + 1) * P], proj[:, :],
                              start=True, stop=True).then_inc(projected, 1)

            @block.scalar
            def _(act):
                for n in range(T // 4):
                    act.wait_ge(transposed, n + 1)
                    act.activation(featT[:, n * BANK:(n + 1) * BANK], banks[n % 2][:, :], ACT.Copy)\
                        .then_inc(T_copied, 1)

            @block.vector
            def _(dve):
                step = Chain(dve, dve0)
                dve.wait_ge(a0_spread, 1)
                dve.wait_ge(a1_turned, 1)
                dve.tensor_copy(a1_cols[:, :], banks[6][:, 0:2])
                w_heads = proj[:, 0:F].rearrange("p (h d) -> p h d", h=H)
                a_heads = banks[7][:, 0:2 * H * D].rearrange("p (h k d) -> p h k d", h=H, k=2)
                for k in range(2):
                    step(dve.tensor_tensor(wa[:, k, :, :], w_heads, a_heads[:, :, k, :], ALU.mult))
                step(dve.reduce_sum(proj[:, F:F + H], wa[:, 1, :, :], axis=AXX))
                dve.reduce_sum(proj[:, F + H:F + 2 * H], wa[:, 0, :, :], axis=AXX).then_inc(proj_ready, 1)
                for t in range(T):
                    dve.wait_ge(projected, t + 1)
                    dve.tensor_copy(values[:, t, :], banks[2 + t % 4][:, 0:F])
                    dve.tensor_copy(scores[:, t, :], banks[2 + t % 4][:, F:F + 2 * H]).then_inc(taken, 1)

        def general_attention(layer, heads, width, d_of, s_of, d_column):
            local = ExitStack()
            with local:
                d_rows = sb(f"d_rows{layer}", [P, heads, N], F32, local)
                adj_tile = sb(f"adj_tile{layer}", [P, N], I32, local)
                keep = sb(f"keep{layer}", [P, N], F32, local)
                away = sb(f"away{layer}", [P, N], F32, local)
                e = sb(f"e{layer}", [P, N], F32, local)
                eT = sb(f"eT{layer}", [P, 2, BANK], F32, local)
                low = sb(f"low{layer}", [P, 4], F32, local)
                spread_ready, spread_done, copied = (sem(f"{n}{layer}") for n in ("spread_ready", "spread_done", "copied"))
                adj_in, adj_used, chain = (sem(f"{n}{layer}") for n in ("adj_in", "adj_used", "dve_g"))
                masked, expd, turned, turned_out, sums, normed = (
                    sem(f"{n}{layer}") for n in ("masked", "expd", "turned", "turned_out", "sums", "normed"))
                B = N // BANK
                with nc.Block() as block:
                    @block.vector
                    def _(dve):
                        for h in range(heads):
                            last = dve.tensor_copy(spread[:, h, :], d_column(h).broadcast_to([P, P]))
                        last.then_inc(spread_ready, 1)
                        for n in range(heads * B):
                            dve.wait_ge(spread_done, n + 1)
                            dve.tensor_copy(d_rows[:, n // B, (n % B) * BANK:(n % B + 1) * BANK], banks[n % 4][:, :])\
                                .then_inc(copied, 1)

                    @block.tensor
                    def _(pe):
                        pe.wait_ge(spread_ready, 1)
                        for n in range(heads * B):
                            if n >= 4:
                                pe.wait_ge(copied, n - 3)
                            pe.matmul(banks[n % 4][:, :], spread[:, n // B, :], featT[:, (n % B) * BANK:(n % B + 1) * BANK],
                                      start=True, stop=True).then_inc(spread_done, 1)

                with nc.Block() as block:
                    @block.sync
                    def _(sp):
                        with sp.Fori(0, T) as it:
                            sp.wait_ge(adj_used, it + 1)
                            sp.dma_start(adj_tile[:, :], adj[bass.ds(it * P, P), :]).then_inc(adj_in, 16)

                    @block.vector
                    def _(dve):
                        dve.memset(low[:, 3:4], 0.0).then_inc(adj_used, 1)
                        with dve.Fori(0, T) as it:
                            dve.wait_ge(adj_in, it * 16 + 16)
                            dve.tensor_scalar(keep[:, :], adj_tile[:, :], 0.0, None, ALU.is_gt).then_inc(chain, 1)
                            dve.tensor_scalar(away[:, :], adj_tile[:, :], 0.0, -NEG_INF, ALU.is_le, ALU.mult)\
                                .then_inc(adj_used, 1)
                            for h in range(heads):
                                q = it * heads + h
                                c = it * (5 * heads + 1) + 5 * h + 1
                                dve.wait_ge(chain, c)
                                dve.tensor_scalar(e[:, :], d_rows[:, h, :], s_of(it, h), None, ALU.add).then_inc(chain, 1)
                                dve.wait_ge(chain, c + 1)
                                dve.scalar_tensor_tensor(out=e[:, :], in0=e[:, :], scalar=SLOPE, in1=e[:, :],
                                                         op0=ALU.mult, op1=ALU.max).then_inc(chain, 1)
                                dve.wait_ge(chain, c + 2)
                                dve.tensor_tensor(e[:, :], e[:, :], keep[:, :], ALU.mult).then_inc(chain, 1)
                                dve.wait_ge(chain, c + 3)
                                dve.wait_ge(adj_used, it + 2)
                                dve.tensor_tensor(e[:, :], e[:, :], away[:, :], ALU.add).then_inc(chain, 1)
                                dve.wait_ge(chain, c + 4)
                                dve.reduce_max(low[:, 0:1], e[:, :], axis=AXX).then_inc(chain, 1)
                                dve.wait_ge(chain, c + 5)
                                dve.tensor_scalar(low[:, 1:2], low[:, 0:1], -1.0, None, ALU.mult).then_inc(masked, 1)
                                dve.wait_ge(expd, q + 1)
                                dve.reciprocal(low[:, 3:4], low[:, 2:3]).then_inc(normed, 1)
                                for n in range(B):
                                    dve.wait_ge(turned, q * B + (n + 1))
                                    dve.tensor_copy(eT[:, n % 2, :], banks[n % 2][:, :]).then_inc(turned_out, 1)
                                dve.wait_ge(sums, q + 1)
                                dve.wait_ge(normed, q + 1)
                                dve.tensor_scalar(summed[:, bass.ds(it, 1), h * width:(h + 1) * width].rearrange("p a w -> p (a w)"),
                                                  banks[2][:, 0:width], low[:, 3:4], None, ALU.mult)

                    @block.scalar
                    def _(act):
                        with act.Fori(0, T) as it:
                            for h in range(heads):
                                act.wait_ge(masked, it * heads + (h + 1))
                                act.activation(e[:, :], e[:, :], ACT.Exp, bias=low[:, 1:2], accum_out=low[:, 2:3])\
                                    .then_inc(expd, 1)

                    @block.tensor
                    def _(pe):
                        with pe.Fori(0, T) as it:
                            for h in range(heads):
                                q = it * heads + h
                                pe.wait_ge(expd, q + 1)

                                def turn(n):
                                    for k in range(4):
                                        j = 4 * n + k
                                        last = pe.transpose(banks[n % 2][:, k * P:(k + 1) * P], e[:, j * P:(j + 1) * P], ident[:, :])
                                    last.then_inc(turned, 1)

                                turn(0)
                                for n in range(B):
                                    if n + 1 < B:
                                        if n >= 1:
                                            pe.wait_ge(turned_out, q * B + n)
                                        turn(n + 1)
                                    pe.wait_ge(turned_out, q * B + (n + 1))
                                    for k in range(4):
                                        j = 4 * n + k
                                        last = pe.matmul(banks[2][:, 0:width], eT[:, n % 2, k * P:(k + 1) * P],
                                                         values[:, j, h * width:(h + 1) * width],
                                                         start=(j == 0), stop=(j == T - 1))
                                last.then_inc(sums, 1)

        general_attention(0, H, D, None, lambda it, h: scores[:, bass.ds(it, 1), H + h:H + h + 1].rearrange("p a b -> p (a b)"),
                          lambda h: proj[:, F + h:F + h + 1])

        tmp = sb("tmp", [P, T, F])
        rows = sb("rows", [P, 12, T])

        def over_rows(ap):
            return ap.rearrange("p (t o) -> p t o", o=1).broadcast_to([P, T, F])

        def layer_norm(step, act_to_do, name, done=None):
            root_asked, root_given = sem(f"{name}_asked"), sem(f"{name}_given")
            mean, var, root, inv = (rows[:, k, :] for k in range(4))
            step(step.engine.reduce_sum(mean, feat[:, :, :], axis=AXX))
            step(step.engine.tensor_scalar(mean, mean, 1.0 / F, None, ALU.mult))
            step(step.engine.tensor_tensor(feat[:, :, :], feat[:, :, :], over_rows(mean), ALU.subtract))
            step(step.engine.tensor_tensor(tmp[:, :, :], feat[:, :, :], feat[:, :, :], ALU.mult))
            step(step.engine.reduce_sum(var, tmp[:, :, :], axis=AXX))
            step.engine.tensor_scalar(var, var, 1.0 / F, LN_EPS, ALU.mult, ALU.add).then_inc(root_asked, 1)
            act_to_do.append((root_asked, root, var, ACT.Sqrt, root_given))
            step.engine.wait_ge(root_given, 1)
            newton_root(step, root, var, inv)
            step(step.engine.reciprocal(inv, root))
            last = step.engine.tensor_tensor(feat[:, :, :], feat[:, :, :], over_rows(inv), ALU.mult)
            if done is None:
                step(last)
            else:
                last.then_inc(done, 1)

        def newton_root(step, root, square, scratch):
            step(step.engine.tensor_scalar(root, root, 1e-30, None, ALU.max))
            step(step.engine.reciprocal(scratch, root))
            step(step.engine.tensor_tensor(scratch, scratch, square, ALU.mult))
            step(step.engine.tensor_tensor(root, root, scratch, ALU.add))
            step(step.engine.tensor_scalar(root, root, 0.5, None, ALU.mult))

        def norm_of(step, act_to_do, name, source, norm, square, scratch):
            asked, given = sem(f"{name}_asked"), sem(f"{name}_given")
            step(step.engine.tensor_tensor(tmp[:, :, :], source, source, ALU.mult))
            step.engine.reduce_sum(square, tmp[:, :, :], axis=AXX).then_inc(asked, 1)
            act_to_do.append((asked, norm, square, ACT.Sqrt, given))
            step.engine.wait_ge(given, 1)
            newton_root(step, norm, square, scratch)

        def serve(act, to_do):
            for asked, to, frm, func, given in to_do:
                act.wait_ge(asked, 1)
                act.activation(to, frm, func).then_inc(given, 1)

        dve1 = sem("dve1")
        elu_low, elu_exp, ln_in, ln_out = sem("elu_low"), sem("elu_exp"), sem("ln_in"), sem("ln_out")
        tan_ready, tan_transposed, tan_T_copied, tan_projected, tan_taken = (
            sem(n) for n in ("tan_ready", "tan_transposed", "tan_T_copied", "tan_projected", "tan_taken"))
        with nc.Block() as block:
            to_do = []

            @block.vector
            def _(dve):
                step = Chain(dve, dve1)
                dve.tensor_scalar(tmp[:, :, :], summed[:, :, :], 0.0, None, ALU.min).then_inc(elu_low, 1)
                to_do.append((elu_low, tmp[:, :, :], tmp[:, :, :], ACT.Exp, elu_exp))
                dve.wait_ge(elu_exp, 1)
                step(dve.scalar_tensor_tensor(out=tmp[:, :, :].rearrange("p t f -> p (t f)"), in0=summed[:, :, :].rearrange("p t f -> p (t f)"), scalar=0.0,
                                              in1=tmp[:, :, :].rearrange("p t f -> p (t f)"), op0=ALU.max, op1=ALU.add))
                step(dve.scalar_tensor_tensor(out=feat[:, :, :].rearrange("p t f -> p (t f)"), in0=tmp[:, :, :].rearrange("p t f -> p (t f)"), scalar=-1.0,
                                              in1=feat[:, :, :].rearrange("p t f -> p (t f)"), op0=ALU.add, op1=ALU.add))
                layer_norm(step, to_do, "ln0")
                norm, square, scratch, plus, minus, ratio, near = (rows[:, k, :] for k in range(7))
                norm_of(step, to_do, "tan_norm", feat[:, :, :], norm, square, scratch)
                step(dve.tensor_scalar(norm, norm, EPS, 1.0 - EPS, ALU.max, ALU.min))
                step(dve.tensor_scalar(plus, norm, 1.0, None, ALU.add))
                dve.tensor_scalar(minus, norm, -1.0, 1.0, ALU.mult, ALU.add).then_inc(ln_in, 1)
                to_do.append((ln_in, rows[:, 3:5, :], rows[:, 3:5, :], ACT.Ln, ln_out))
                dve.wait_ge(ln_out, 1)
                step(dve.tensor_tensor(ratio, plus, minus, ALU.subtract))
                step(dve.reciprocal(scratch, norm))
                step(dve.tensor_tensor(ratio, ratio, scratch, ALU.mult))
                step(dve.tensor_scalar(ratio, ratio, 0.5, None, ALU.mult))
                step(dve.tensor_tensor(square, norm, norm, ALU.mult))
                step(dve.tensor_scalar(near, square, 1.0 / 9, 1.0 / 7, ALU.mult, ALU.add))
                for c in (5, 3, 1):
                    step(dve.tensor_tensor(near, near, square, ALU.mult))
                    step(dve.tensor_scalar(near, near, 1.0 / c, None, ALU.add))
                step(dve.tensor_tensor(near, near, ratio, ALU.subtract))
                step(dve.tensor_scalar(scratch, norm, 0.1, None, ALU.is_lt))
                step(dve.tensor_tensor(near, near, scratch, ALU.mult))
                step(dve.tensor_tensor(ratio, ratio, near, ALU.add))
                dve.tensor_tensor(values[:, :, :], feat[:, :, :], over_rows(ratio), ALU.mult).then_inc(tan_ready, 1)
                dve.wait_ge(tan_T_copied, T // 4)
                for t in range(T):
                    dve.wait_ge(tan_projected, t + 1)
                    dve.tensor_copy(scores[:, t, 0:2], banks[2 + t % 4][:, 0:2]).then_inc(tan_taken, 1)

            @block.scalar
            def _(act):
                serve(act, to_do)
                for n in range(T // 4):
                    act.wait_ge(tan_transposed, n + 1)
                    act.activation(featT[:, n * BANK:(n + 1) * BANK], banks[n % 2][:, :], ACT.Copy)\
                        .then_inc(tan_T_copied, 1)

            @block.tensor
            def _(pe):
                pe.wait_ge(tan_ready, 1)
                for n in range(T // 4):
                    if n >= 2:
                        pe.wait_ge(tan_T_copied, n - 1)
                    for t in range(4 * n, 4 * n + 4):
                        last = pe.transpose(banks[n % 2][:, (t % 4) * P:(t % 4 + 1) * P], values[:, t, :], ident[:, :])
                    last.then_inc(tan_transposed, 1)
                pe.wait_ge(tan_T_copied, T // 4)
                for t in range(T):
                    if t >= 4:
                        pe.wait_ge(tan_taken, t - 3)
                    pe.matmul(banks[2 + t % 4][:, 0:2], featT[:, t * P:(t + 1) * P], a1_cols[:, :],
                              start=True, stop=True).then_inc(tan_projected, 1)

        general_attention(1, 1, F, None, lambda it, h: scores[:, bass.ds(it, 1), 0:1].rearrange("p a b -> p (a b)"),
                          lambda h: a1_cols[:, 1:2])

        dve2, done, stored = sem("dve2"), sem("done"), sem("stored")
        tanh_in, tanh_out = sem("tanh_in"), sem("tanh_out")
        with nc.Block() as block:
            to_do1 = []

            @block.vector
            def _(dve):
                step = Chain(dve, dve2)
                raw, square, scratch, norm, gain, big = (rows[:, k, :] for k in range(6))
                norm_of(step, to_do1, "exp_norm", summed[:, :, :], raw, square, scratch)
                dve.tensor_scalar(norm, raw, EPS, None, ALU.max).then_inc(tanh_in, 1)
                to_do1.append((tanh_in, gain, norm, ACT.Tanh, tanh_out))
                dve.wait_ge(tanh_out, 1)
                step(dve.reciprocal(scratch, norm))
                step(dve.tensor_tensor(gain, gain, scratch, ALU.mult))
                step(dve.tensor_tensor(norm, gain, raw, ALU.mult))
                step(dve.tensor_scalar(norm, norm, EPS, None, ALU.max))
                step(dve.tensor_scalar(big, norm, MAX_NORM, None, ALU.is_gt))
                step(dve.reciprocal(scratch, norm))
                step(dve.tensor_scalar(scratch, scratch, MAX_NORM, -1.0, ALU.mult, ALU.add))
                step(dve.tensor_tensor(scratch, scratch, big, ALU.mult))
                step(dve.tensor_scalar(scratch, scratch, 1.0, None, ALU.add))
                step(dve.tensor_tensor(gain, gain, scratch, ALU.mult))
                step(dve.tensor_tensor(tmp[:, :, :], summed[:, :, :], over_rows(gain), ALU.mult))
                step(dve.tensor_tensor(feat[:, :, :], feat[:, :, :], tmp[:, :, :], ALU.add))
                layer_norm(step, to_do1, "ln1", done)

            @block.scalar
            def _(act):
                serve(act, to_do1)

            @block.sync
            def _(sp):
                sp.wait_ge(done, 1)
                sp.dma_start(out_rows, feat[:, :, :]).then_inc(stored, 16)
                sp.wait_ge(stored, 16)


_INS = ['x', 'adj', 'L0_gnn_W', 'L0_gnn_a', 'L1_gnn_a']
_OUTS = [((4096, 128), 'float32')]


def kernel(**inputs):
    import numpy as _np
    import concourse.bacc as _bacc
    from concourse import mybir as _mybir
    from concourse.bass_utils import run_bass_kernel_spmd as _run

    nc = _bacc.Bacc("TRN2", target_bir_lowering=False, num_devices=1)
    arrays, args = {}, []
    for name in _INS:
        a = _np.ascontiguousarray(inputs[name])
        arrays[f"in_{name}_dram"] = a
        args.append(nc.dram_tensor(f"in_{name}_dram", a.shape, _mybir.dt.from_np(a.dtype), kind="ExternalInput").ap())
    for i, (shape, dtype) in enumerate(_OUTS):
        dt = _mybir.dt.from_np(_np.dtype(dtype))
        args.append(nc.dram_tensor(f"out_{i}_dram", shape, dt, kind="ExternalOutput").ap())
    two_layer_gat(nc, *args)
    r = _run(nc, [arrays], core_ids=[0])
    return r.results[0]["out_0_dram"]
```

```python
import concourse.bass as bass
from concourse import mybir
from contextlib import ExitStack


F32, BF16, FP8, I32, U8 = (mybir.dt.float32, mybir.dt.bfloat16, mybir.dt.float8e4, mybir.dt.int32, mybir.dt.uint8)
ALU = mybir.AluOpType
ACT = mybir.ActivationFunctionType
AXX = mybir.AxisListType.X

P = 128
SLOPE = 0.2
NEG_INF = 9.0e15
EPS = 1e-7
MAX_NORM = 1.0 - 0.001
LN_EPS = 1e-5
BANK = 512
PARTS = 3
TWO = 0x40
TWOS = 0x40404040

WIDEST = 142.0
WIDEST_ALL = 150.0
LARGEST_SCORE = 300.0
LARGEST_VALUE = 490.0
CENTRE_SHIFT = 3.0
LARGEST_EXPONENT = 80.0


class Chain:

    def __init__(self, engine, semaphore, before=0):
        self.engine, self.semaphore, self.before, self.count = engine, semaphore, before, 0

    def __call__(self, instruction):
        self.count += 1
        instruction.then_inc(self.semaphore, 1)
        self.engine.wait_ge(self.semaphore, self.before + self.count)


def two_layer_gat(nc, x, adj, W, a0, a1, out):
    N, F = x.shape
    H, D = a0.shape[1], a0.shape[2] // 2
    T = N // P
    x_rows = x.rearrange("(t p) f -> p t f", p=P)
    out_rows = out.rearrange("(t p) f -> p t f", p=P)

    CT = 8
    C = CT * P
    NC = T // CT
    JU = 4
    UH = T // JU
    U = H * UH
    NB = CT // 2
    SLOTS = 4
    K0 = D + 1
    K1 = F + 1
    W0 = 2 * PARTS * K0
    ON_ACT = [True, False, True, False, True, True, False, True]
    NA, ND = H * sum(ON_ACT), H * (UH - sum(ON_ACT))
    GQ = 8
    QT = T // GQ
    Q = CT * QT
    FIRST_STEP, LAST_STEP = 8, 27
    ROT = 8
    ON_POOL = 2
    LAG = 3

    def groups_at(u):
        if not FIRST_STEP <= u <= LAST_STEP:
            return range(0)
        n = LAST_STEP - FIRST_STEP + 1
        k = u - FIRST_STEP
        return range(k * Q // n, (k + 1) * Q // n)

    RT = 4
    R = RT * P
    NR = T // RT

    score_rows = nc.dram_tensor("score_rows", (2 * H, N), F32, kind="Internal").ap()
    score_rows1 = nc.dram_tensor("score_rows1", (2, N), F32, kind="Internal").ap()
    values_kept = nc.dram_tensor("values_kept", (P, T, F), F32, kind="Internal").ap()
    masks_kept = nc.dram_tensor("masks_kept", (NC, P, T, C // 4), I32, kind="Internal").ap()

    ctx = ExitStack()
    with ctx:
        def sb(name, shape, dt=F32, where=ctx):
            return where.enter_context(nc.sbuf_tensor(name, shape, dt))

        def sem(name):
            return ctx.enter_context(nc.semaphore(name))

        def sems(*names):
            return [sem(n) for n in names]

        def hold(engine, semaphore, value):
            engine.wait_ge(semaphore, value)
            if not isinstance(value, int):
                engine.sem_inc(passed, 1)

        passed = sem("passed")

        def one(ap):
            return ap.rearrange("p a b -> p (a b)")

        ident = sb("ident", [P, P])
        feat = sb("feat", [P, T, F])
        a1_spread = sb("a1_spread", [P, 2, F])
        scores = sb("scores", [P, T, 2 * H])
        work = sb("work", [P, CT, F])
        stats = sb("stats", [P, CT, 8])
        mean_var = sb("mean_var", [P, CT, 2])
        var = sb("var", [P, T])
        dots = sb("dots", [P, 2, T])
        flag = sb("flag", [1, 1], I32)
        flag1 = sb("flag1", [1, 1], I32)
        factors = sb("factors", [P, H, T, 2])
        mean_values = sb("mean_values", [P, F])
        bank = [ctx.enter_context(nc.psum_tensor(f"bank{i}", [P, BANK], F32)) for i in range(8)]


        def bounds(step, H, seen, column, spread_bank, low, centre, flag_out, turned, given):
            e = step.engine
            e.wait_ge(turned, 1)
            step(e.reduce_max(column[0:4 * H + 2, :], spread_bank[0:4 * H + 2, 0:P], axis=AXX))
            e.tensor_scalar(seen[0:4 * H + 2, 0:4 * H + 2], ident[0:4 * H + 2, 0:4 * H + 2],
                            column[0:4 * H + 2, 0:1], None, ALU.mult).then_inc(given, 1)
            e.wait_ge(turned, 2)
            b = seen
            step(e.tensor_copy(b[:, 0:4 * H + 2], spread_bank[:, P:P + 4 * H + 2]))
            d_max, s_max, d_min, s_min = (b[:, k * H:(k + 1) * H] for k in range(4))
            step(e.tensor_tensor(low, d_min, s_max, ALU.min))
            step(e.tensor_scalar(centre, d_max, -1.0, None, ALU.mult))
            step(e.tensor_tensor(low, low, centre, ALU.max))
            step(e.tensor_tensor(centre, d_max, low, ALU.subtract))
            step(e.tensor_scalar(centre, centre, 0.5, -CENTRE_SHIFT, ALU.mult, ALU.add))
            w = b[:, 4 * H + 2:5 * H + 2]
            w_all = b[:, 5 * H + 2:6 * H + 2]
            step(e.tensor_tensor(w, d_max, low, ALU.add))
            step(e.tensor_scalar(w, w, 1.0 / WIDEST, None, ALU.mult))
            step(e.tensor_tensor(w_all, d_max, d_min, ALU.add))
            step(e.tensor_scalar(w_all, w_all, 1.0 / WIDEST_ALL, None, ALU.mult))
            step(e.tensor_scalar(b[:, 0:4 * H], b[:, 0:4 * H], 1.0 / LARGEST_SCORE, None, ALU.mult))
            step(e.tensor_scalar(b[:, 4 * H:4 * H + 2], b[:, 4 * H:4 * H + 2], 1.0 / LARGEST_VALUE, None, ALU.mult))
            step(e.reduce_max(column[:, :], b[:, 0:6 * H + 2], axis=AXX))
            step(e.tensor_scalar(flag_out[0:1, 0:1], column[0:1, 0:1], 1.0, None, ALU.is_gt))
            step(e.tensor_scalar(low, low, -1.0, None, ALU.mult))

        def exponents(step, exp_asked, H, d_of, s_of, low, centre, up, down, rows, negative_d):
            e = step.engine
            for h in range(H):
                e.tensor_scalar(up[:, h, :], d_of(h), low[:, h:h + 1], centre[:, h:h + 1], ALU.max, ALU.subtract)
                e.tensor_scalar(down[:, h, :], d_of(h), SLOPE, None, ALU.mult)
                e.tensor_scalar(negative_d[:, h, :], d_of(h), -1.0, None, ALU.mult)
                step(e.tensor_scalar(rows[:, h, :, 0], s_of(h), 1.0 - SLOPE, centre[:, h:h + 1], ALU.mult, ALU.add))
                step(e.tensor_scalar(rows[:, h, :, 1], rows[:, h, :, 0], -1.0, 0.0, ALU.mult, ALU.min))
                step(e.tensor_scalar(rows[:, h, :, 0], rows[:, h, :, 0], 0.0, None, ALU.min))
            e.tensor_scalar(up[:, :, :], up[:, :, :], LARGEST_EXPONENT, None, ALU.min)
            e.tensor_scalar(down[:, :, :], down[:, :, :], LARGEST_EXPONENT, None, ALU.min).then_inc(exp_asked, 1)

        def split(step, source, high, middle, lowest):
            e = step.engine
            step(e.tensor_copy(high, source))
            step(e.tensor_tensor(source, source, high, ALU.subtract))
            step(e.tensor_copy(middle, source))
            step(e.tensor_tensor(lowest, source, middle, ALU.subtract))

        def newton_root(step, root, square, scratch):
            e = step.engine
            step(e.tensor_scalar(root, root, 1e-30, None, ALU.max))
            step(e.reciprocal(scratch, root))
            step(e.tensor_tensor(scratch, scratch, square, ALU.mult))
            step(e.tensor_tensor(root, root, scratch, ALU.add))
            step(e.tensor_scalar(root, root, 0.5, None, ALU.mult))

        WEIGH = 7

        def weigh(dve, done, before, sides, mixed, empty, inverse, factors, mean, width, tiles, out):
            step = Chain(dve, done, before)
            flat = sides[:, :, :, :].rearrange("p t b k -> p (t b) k")
            step(dve.tensor_tensor(flat, flat, factors.rearrange("p t (b o) -> p (t b) o", o=1)
                                   .broadcast_to([P, 2 * tiles, width + 1]), ALU.mult))
            step(dve.tensor_tensor(mixed[:, :, :], sides[:, :, 0, :], sides[:, :, 1, :], ALU.add))
            none = inverse[:, 0, :].rearrange("p (t o) -> p t o", o=1)
            inv = inverse[:, 1, :].rearrange("p (t o) -> p t o", o=1)
            total = mixed[:, :, width:width + 1]
            step(dve.tensor_scalar(none, total, 0.0, None, ALU.is_equal))
            step(dve.tensor_tensor(inv, total, none, ALU.add))
            step(dve.tensor_tensor(empty[:, :, :], none.broadcast_to([P, tiles, width]),
                                   mean.rearrange("p (o k) -> p o k", o=1).broadcast_to([P, tiles, width]), ALU.mult))
            dve.tensor_tensor(mixed[:, :, 0:width], mixed[:, :, 0:width], empty[:, :, :], ALU.add)
            step(dve.reciprocal(inv, inv))
            step(dve.tensor_tensor(out, mixed[:, :, 0:width], inv.broadcast_to([P, tiles, width]), ALU.mult))
            assert step.count == WEIGH

        def general_attention(layer, heads, width, flag_ap, d_rows_dram, s_of, values_in, summed, finish):
            local = ExitStack()
            with local:
                v = values_in
                if v is None:
                    v = sb(f"g_values{layer}", [P, T, F], F32, local)
                d_rows = sb(f"d_rows{layer}", [P, heads, N], F32, local)
                adj_tile = sb(f"adj_tile{layer}", [P, N], I32, local)
                keep = sb(f"keep{layer}", [P, N], F32, local)
                away = sb(f"away{layer}", [P, N], F32, local)
                e = sb(f"e{layer}", [P, N], F32, local)
                eT = sb(f"eT{layer}", [P, 2, BANK], F32, local)
                rowwise = sb(f"rowwise{layer}", [P, 4], F32, local)
                loaded, adj_in, adj_used, chain = sems(*(f"g_{n}{layer}" for n in ("loaded", "adj_in", "adj_used", "chain")))
                masked, expd, turned, turned_out, sums, normed, given = sems(
                    *(f"g_{n}{layer}" for n in ("masked", "expd", "turned", "turned_out", "sums", "normed", "given")))
                B = N // BANK
                with nc.Block() as block:
                    @block.sync
                    def _(sp):
                        with sp.If(sp.value_load(flag_ap, min_val=0, max_val=1) > 0):
                            sp.dma_start(d_rows[:, :, :], d_rows_dram.rearrange("(o h) n -> o h n", o=1)
                                         .broadcast_to([P, heads, N])).then_inc(loaded, 16)
                            if values_in is None:
                                sp.dma_start(v[:, :, :], values_kept).then_inc(loaded, 16)
                            with sp.Fori(0, T) as it:
                                sp.wait_ge(adj_used, it + 1)
                                sp.dma_start(adj_tile[:, :], adj[bass.ds(it * P, P), :]).then_inc(adj_in, 16)

                    @block.vector
                    def _(dve):
                        with dve.If(dve.value_load(flag_ap, min_val=0, max_val=1) > 0):
                            dve.memset(rowwise[:, 3:4], 0.0).then_inc(adj_used, 1)
                            dve.wait_ge(loaded, 16 if values_in is not None else 32)
                            with dve.Fori(0, T) as it:
                                dve.wait_ge(adj_in, it * 16 + 16)
                                dve.tensor_scalar(keep[:, :], adj_tile[:, :], 0.0, None, ALU.is_gt).then_inc(chain, 1)
                                dve.tensor_scalar(away[:, :], adj_tile[:, :], 0.0, -NEG_INF, ALU.is_le, ALU.mult)\
                                    .then_inc(adj_used, 1)
                                for h in range(heads):
                                    q = it * heads + h
                                    c = it * (5 * heads + 1) + 5 * h + 1
                                    dve.wait_ge(chain, c)
                                    dve.tensor_scalar(e[:, :], d_rows[:, h, :], s_of(it, h), None, ALU.add).then_inc(chain, 1)
                                    dve.wait_ge(chain, c + 1)
                                    dve.scalar_tensor_tensor(out=e[:, :], in0=e[:, :], scalar=SLOPE, in1=e[:, :],
                                                             op0=ALU.mult, op1=ALU.max).then_inc(chain, 1)
                                    dve.wait_ge(chain, c + 2)
                                    dve.tensor_tensor(e[:, :], e[:, :], keep[:, :], ALU.mult).then_inc(chain, 1)
                                    dve.wait_ge(chain, c + 3)
                                    dve.wait_ge(adj_used, it + 2)
                                    dve.tensor_tensor(e[:, :], e[:, :], away[:, :], ALU.add).then_inc(chain, 1)
                                    dve.wait_ge(chain, c + 4)
                                    dve.reduce_max(rowwise[:, 0:1], e[:, :], axis=AXX).then_inc(chain, 1)
                                    dve.wait_ge(chain, c + 5)
                                    dve.tensor_scalar(rowwise[:, 1:2], rowwise[:, 0:1], -1.0, None, ALU.mult)\
                                        .then_inc(masked, 1)
                                    dve.wait_ge(expd, q + 1)
                                    dve.reciprocal(rowwise[:, 3:4], rowwise[:, 2:3]).then_inc(normed, 1)
                                    for n in range(B):
                                        dve.wait_ge(turned, q * B + (n + 1))
                                        dve.tensor_copy(eT[:, n % 2, :], bank[n % 2][:, :]).then_inc(turned_out, 1)
                                    dve.wait_ge(sums, q + 1)
                                    dve.wait_ge(normed, q + 1)
                                    dve.tensor_scalar(one(summed[:, bass.ds(it, 1), h * width:(h + 1) * width]),
                                                      bank[2][:, 0:width], rowwise[:, 3:4], None, ALU.mult)\
                                        .then_inc(given, 1)
                            dve.wait_ge(given, T * heads)
                            finish(dve, None)

                    @block.scalar
                    def _(act):
                        with act.If(act.value_load(flag_ap, min_val=0, max_val=1) > 0):
                            with act.Fori(0, T) as it:
                                for h in range(heads):
                                    act.wait_ge(masked, it * heads + (h + 1))
                                    act.activation(e[:, :], e[:, :], ACT.Exp, bias=rowwise[:, 1:2],
                                                   accum_out=rowwise[:, 2:3]).then_inc(expd, 1)
                            finish(None, act)

                    @block.tensor
                    def _(pe):
                        with pe.If(pe.value_load(flag_ap, min_val=0, max_val=1) > 0):
                            pe.wait_ge(loaded, 16 if values_in is not None else 32)
                            with pe.Fori(0, T) as it:
                                for h in range(heads):
                                    q = it * heads + h
                                    pe.wait_ge(expd, q + 1)

                                    def turn(n):
                                        for k in range(4):
                                            j = 4 * n + k
                                            last = pe.transpose(bank[n % 2][:, k * P:(k + 1) * P],
                                                                e[:, j * P:(j + 1) * P], ident[:, :])
                                        last.then_inc(turned, 1)

                                    turn(0)
                                    for n in range(B):
                                        if n + 1 < B:
                                            if n >= 1:
                                                pe.wait_ge(turned_out, q * B + n)
                                            turn(n + 1)
                                        pe.wait_ge(turned_out, q * B + (n + 1))
                                        for k in range(4):
                                            j = 4 * n + k
                                            last = pe.matmul(bank[2][:, 0:width], eT[:, n % 2, k * P:(k + 1) * P],
                                                             v[:, j, h * width:(h + 1) * width],
                                                             start=(j == 0), stop=(j == T - 1))
                                    last.then_inc(sums, 1)

        elu_asked, elu_given, fin = sems("elu_asked", "elu_given", "fin")
        fast0 = ExitStack()
        moving = sb("moving", [P, T, H, W0], BF16, fast0)
        masks = sb("masks", [P, T * C], FP8, fast0)
        raw_masks = sb("raw_masks", [P, T * C], FP8, fast0)
        ring = sb("ring", [P, SLOTS, 2, JU * C], FP8, fast0)
        adj_tiles = sb("adj_tiles", [P, 2, N], BF16, fast0)
        s_rows = sb("s_rows", [P, 2, C], F32, fast0)
        ident_b = sb("ident_b", [P, P], BF16, fast0)
        neg_d = sb("neg_d", [P, H, T], F32, fast0)
        evac = sb("evac", [P, CT, 2, K0], F32, fast0)
        mixed = sb("mixed", [P, CT, K0], F32, fast0)
        empty = sb("empty", [P, CT, D], F32, fast0)
        attended = sb("attended", [P, CT, F], F32, fast0)
        inverse = sb("inverse", [P, 2, CT], F32, fast0)
        low0 = sb("low0", [P, H], F32, fast0)
        centre0 = sb("centre0", [P, H], F32, fast0)
        above_d, below_d = (sb(n, [P, H, T], F32, fast0) for n in ("above_d", "below_d"))

        idle = masks[:, :].bitcast(F32)
        featT = idle[:, 0:N]
        values = idle[:, N:2 * N].rearrange("p (t f) -> p t f", f=F)
        spare = ring[:, :, :, :].rearrange("p s b n -> p (s b n)").bitcast(F32)
        proj = spare[:, 0:F + 2 * H]
        wa = spare[:, 256:256 + 2 * F].rearrange("p (k h d) -> p k h d", k=2, h=H)
        a_row = spare[0:1, 512:512 + 2 * F]
        a1_row = spare[0:1, 768:768 + 2 * F]
        ones = spare[:, 1024:1024 + P]
        seen = spare[:, 1152:1152 + 6 * H + 2]
        column = spare[:, 1200:1201]
        turned_scores = spare[0:T, 1280:1280 + 2 * H * P].rearrange("t (k p) -> t k p", k=2 * H)
        part_b = spare[:, 2560:2560 + T * K0].rearrange("p (t k) -> p t k", k=K0)
        part_d = spare[:, 3840:3840 + T * K0].rearrange("p (t k) -> p t k", k=K0)
        all_columns = moving[:, :, :, :].rearrange("p t h (b q k) -> p t h b q k", b=2, q=PARTS)

        x_in, small_in, ident_zero, ident_ready, ones_ready, ident_b_ready = sems(
            "x_in", "small_in", "ident_zero", "ident_ready", "ones_ready", "ident_b_ready")
        a_spread, dve0, pool0, proj_ready, transposed, T_copied, projected, taken = sems(
            "a_spread", "dve0", "pool0", "proj_ready", "transposed", "T_copied", "projected", "taken")
        extrema_ready, extrema_turned, extrema_given, scores_turned, scores_copied = sems(
            "extrema_ready", "extrema_turned", "extrema_given", "scores_turned", "scores_copied")
        mean_ready, exp_asked, exp_given, scores_out, values_out = sems(
            "mean_ready", "exp_asked", "exp_given", "scores_out", "values_out")
        adj_in = sems("adj_in0", "adj_in1")
        a1_taken, turned, turned_out, mask_ready, kept, pool_done = sems(
            "a1_taken", "turned", "turned_out", "mask_ready", "kept", "pool_done")
        s_in = sems("s_head_in0", "s_head_in1")
        s_read_act, s_read_dve = sems("s_read_act", "s_read_dve")
        signs_ready, compared, below_ready, unit_ready, unit_done, acc_ready, acc_taken = sems(
            "signs_ready", "compared", "below_ready", "unit_ready", "unit_done", "acc_ready", "acc_taken")

        turn_bank = [bank[4 + i] for i in range(4)]

        def load_adj(pool, b, t):
            pool.dma_start(adj_tiles[:, t % 2, :], adj[bass.ds(b * C + t * P, P), :]).then_inc(adj_in[t % 2], 16)

        def turn_group(pe, b, q):
            t = q // QT
            if q % QT == 0:
                pe.wait_ge(adj_in[t % 2], b * (8 * CT) + 16 * (t // 2 + 1))
            if isinstance(b, int) and b == 0 and q < 4:
                pass
            else:
                hold(pe, turned_out, b * Q + (q - 3))
            dst = turn_bank[q % 4][:, :].bitcast(BF16)
            for k in range(GQ):
                j = (q % QT) * GQ + k
                last = pe.transpose(dst[:, k * P:(k + 1) * P], adj_tiles[:, t % 2, j * P:(j + 1) * P], ident_b[:, :])
            last.then_inc(turned, 1)

        def take_group(act, b, q):
            t, j = q // QT, (q % QT) * GQ
            hold(act, turned, b * Q + (q + 1))
            dst = raw_masks[:, :].rearrange("p (j i) -> p j i", i=C)
            act.activation(dst[:, j:j + GQ, t * P:(t + 1) * P],
                           turn_bank[q % 4][:, :].bitcast(BF16).rearrange("p (j i) -> p j i", i=P),
                           ACT.Relu, scale=2.0, saturate=False).then_inc(turned_out, 1)

        def two_tiles(n):
            return bank[2 + n % 2][:, 0:2 * (F + 2 * H)].rearrange("p (t k) -> p t k", t=2)

        def groups_of(n):
            return range(n, n + 1)

        def weigh_values(step, part, h, b, weight):
            weight = weight[:, h, :].rearrange("p (t o) -> p t o", o=1)
            step(step.engine.tensor_tensor(part[:, :, 0:D], values[:, :, h * D:(h + 1) * D],
                                           weight.broadcast_to([P, T, D]), ALU.mult))
            step(step.engine.tensor_copy(part[:, :, D:K0], weight))
            split(step, part, *(all_columns[:, :, h, b, q, :] for q in range(PARTS)))

        def clean_masks(dve, b):
            dve.wait_ge(turned_out, b * Q + Q)
            dve.tensor_scalar(masks[:, :].bitcast(I32), raw_masks[:, :].bitcast(I32), TWOS, None, ALU.bitwise_and)\
                .then_inc(mask_ready, 1)

        with nc.Block() as block:
            @block.sync
            def _(sp):
                sp.dma_start(proj[:, 0:F], W).then_inc(small_in, 16)
                sp.dma_start(a_row, a0.rearrange("o h e -> o (h e)")).then_inc(small_in, 16)
                sp.dma_start(a1_row, a1.rearrange("f o -> o f")).then_inc(small_in, 16)
                sp.dma_start(feat[:, :, :], x_rows).then_inc(x_in, 16)
                sp.wait_ge(taken, T // 2)
                sp.dma_start(values_kept, values).then_inc(values_out, 16)
                sp.wait_ge(scores_copied, 1)
                sp.dma_start(score_rows.rearrange("k (t p) -> t k p", p=P), turned_scores).then_inc(scores_out, 16)
                sp.wait_ge(scores_out, 16)
                for h in range(2):
                    sp.dma_start(s_rows[:, h, :], score_rows[H + h:H + h + 1, 0:C].broadcast_to([P, C]))\
                        .then_inc(s_in[h], 16)
                sp.wait_ge(values_out, 16)
                for h in range(2):
                    sp.wait_ge(s_in[h], 16)

            @block.gpsimd
            def _(pool):
                pool.memset(ones, 1.0).then_inc(ones_ready, 1)
                pool.memset(ident[:, :], 0.0).then_inc(ident_zero, 1)
                pool.wait_ge(ident_zero, 1)
                pool.affine_select(out=ident[:, :], in_=ident[:, :], compare_op=ALU.not_equal, fill=1.0, base=0,
                                   pattern=[[-1, P]], channel_multiplier=1).then_inc(ident_ready, 1)
                load_adj(pool, 0, 0)
                load_adj(pool, 0, 1)
                pool.wait_ge(ident_ready, 1)
                pool.tensor_copy(ident_b[:, :], ident[:, :]).then_inc(ident_b_ready, 1)
                for t in range(2, CT):
                    pool.wait_ge(turned, (t - 1) * QT)
                    load_adj(pool, 0, t)
                step = Chain(pool, pool0)
                pool.wait_ge(exp_given, 2)
                for h in range(H - ON_POOL, H):
                    weigh_values(step, part_d, h, 1, below_d)
                pool.sem_inc(pool_done, 1)

            @block.tensor
            def _(pe):
                pe.wait_ge(small_in, 48)
                pe.wait_ge(ones_ready, 1)
                pe.matmul(bank[2][:, 0:2 * F], ones[0:1, :], a_row, start=True, stop=True)
                pe.matmul(bank[3][:, 0:2 * F], ones[0:1, :], a1_row, start=True, stop=True).then_inc(a_spread, 1)
                pe.wait_ge(x_in, 16)
                pe.wait_ge(ident_ready, 1)
                for n in range(T // 4):
                    if n >= 2:
                        pe.wait_ge(T_copied, n - 1)
                    for t in range(4 * n, 4 * n + 4):
                        last = pe.transpose(bank[n % 2][:, (t % 4) * P:(t % 4 + 1) * P], feat[:, t, :], ident[:, :])
                    last.then_inc(transposed, 1)
                pe.wait_ge(proj_ready, 1)
                pe.wait_ge(a1_taken, 1)
                pe.wait_ge(ident_b_ready, 1)
                for n in range(T // 2):
                    if n % 2 == 0:
                        pe.wait_ge(T_copied, n // 2 + 1)
                    if n >= 2:
                        pe.wait_ge(taken, n - 1)
                    for t in range(2 * n, 2 * n + 2):
                        at = (t % 2) * (F + 2 * H)
                        last = pe.matmul(bank[2 + n % 2][:, at:at + F + 2 * H], featT[:, t * P:(t + 1) * P], proj,
                                         start=True, stop=True)
                    last.then_inc(projected, 1)
                    for q in groups_of(n):
                        turn_group(pe, 0, q)
                pe.wait_ge(taken, T // 2)
                for t in range(T):
                    last = pe.matmul(bank[2][:, 0:F], ones, values[:, t, :], start=(t == 0), stop=(t == T - 1))
                last.then_inc(mean_ready, 1)
                for k in range(2 * H):
                    last = pe.transpose(bank[k // 4][0:T, (k % 4) * P:(k % 4 + 1) * P], scores[:, :, k], ident[:, :])
                last.then_inc(scores_turned, 1)
                pe.wait_ge(extrema_ready, 1)
                pe.transpose(bank[3][0:4 * H + 2, 0:P], seen[:, 0:4 * H + 2], ident[:, :]).then_inc(extrema_turned, 1)
                pe.wait_ge(extrema_given, 1)
                pe.matmul(bank[3][:, P:P + 4 * H + 2], ones[0:4 * H + 2, :], seen[0:4 * H + 2, 0:4 * H + 2],
                          start=True, stop=True).then_inc(extrema_turned, 1)
                for q in range(T // 2, Q):
                    turn_group(pe, 0, q)

            @block.scalar
            def _(act):
                for n in range(T // 4):
                    act.wait_ge(transposed, n + 1)
                    act.activation(featT[:, n * BANK:(n + 1) * BANK], bank[n % 2][:, :], ACT.Copy)\
                        .then_inc(T_copied, 1)
                for n in range(T // 2):
                    for q in groups_of(n):
                        take_group(act, 0, q)
                act.wait_ge(scores_turned, 1)
                for k in range(2):
                    last = act.activation(turned_scores[:, 4 * k:4 * k + 4, :].rearrange("t k p -> t (k p)"),
                                          bank[k][0:T, :], ACT.Copy)
                last.then_inc(scores_copied, 1)
                act.wait_ge(exp_asked, 1)
                act.activation(above_d[:, :, :], above_d[:, :, :], ACT.Exp).then_inc(exp_given, 1)
                act.activation(below_d[:, :, :], below_d[:, :, :], ACT.Exp).then_inc(exp_given, 1)
                act.activation(factors[:, :, :, :], factors[:, :, :, :], ACT.Exp).then_inc(exp_given, 1)
                for q in range(T // 2, Q):
                    take_group(act, 0, q)

            @block.vector
            def _(dve):
                step = Chain(dve, dve0)
                dve.wait_ge(a_spread, 1)
                w_heads = proj[:, 0:F].rearrange("p (h d) -> p h d", h=H)
                a_heads = bank[2][:, 0:2 * F].rearrange("p (h k d) -> p h k d", h=H, k=2)
                for k in range(2):
                    step(dve.tensor_tensor(wa[:, k, :, :], w_heads, a_heads[:, :, k, :], ALU.mult))
                step(dve.reduce_sum(proj[:, F:F + H], wa[:, 1, :, :], axis=AXX))
                dve.reduce_sum(proj[:, F + H:F + 2 * H], wa[:, 0, :, :], axis=AXX).then_inc(proj_ready, 1)
                dve.tensor_copy(a1_spread[:, :, :].rearrange("p k f -> p (k f)"), bank[3][:, 0:2 * F])\
                    .then_inc(a1_taken, 1)
                for n in range(T // 2):
                    dve.wait_ge(projected, n + 1)
                    dve.tensor_copy(values[:, 2 * n:2 * n + 2, :], two_tiles(n)[:, :, 0:F])
                    dve.tensor_copy(scores[:, 2 * n:2 * n + 2, :], two_tiles(n)[:, :, F:F + 2 * H]).then_inc(taken, 1)
                dve.wait_ge(taken, T // 2)
                by_kind = scores[:, :, :].rearrange("p t k -> p k t")
                flat_values = values.rearrange("p t f -> p (t f)")
                dve.tensor_reduce(seen[:, 0:2 * H], by_kind, axis=AXX, op=ALU.max)
                dve.tensor_reduce(seen[:, 2 * H:4 * H], by_kind, axis=AXX, op=ALU.min)
                dve.tensor_reduce(seen[:, 4 * H:4 * H + 1], flat_values, axis=AXX, op=ALU.max)
                step(dve.tensor_reduce(seen[:, 4 * H + 1:4 * H + 2], flat_values, axis=AXX, op=ALU.min))
                step(dve.tensor_scalar(seen[:, 2 * H:4 * H], seen[:, 2 * H:4 * H], -1.0, None, ALU.mult))
                dve.tensor_scalar(seen[:, 4 * H + 1:4 * H + 2], seen[:, 4 * H + 1:4 * H + 2], -1.0, None, ALU.mult)\
                    .then_inc(extrema_ready, 1)
                dve.wait_ge(mean_ready, 1)
                step(dve.tensor_scalar(mean_values[:, :], bank[2][:, 0:F], 1.0 / N, None, ALU.mult))
                bounds(step, H, seen, column, bank[3], low0[:, :], centre0[:, :], flag, extrema_turned, extrema_given)
                exponents(step, exp_asked, H, lambda h: scores[:, :, h], lambda h: scores[:, :, H + h],
                          low0[:, :], centre0[:, :], above_d, below_d, factors, neg_d)
                dve.wait_ge(exp_given, 1)
                for h in range(H):
                    weigh_values(step, part_b, h, 0, above_d)
                dve.wait_ge(exp_given, 2)
                for h in range(H - ON_POOL):
                    weigh_values(step, part_b, h, 1, below_d)
                dve.wait_ge(exp_given, 3)
                dve.wait_ge(pool_done, 1)
                dve.wait_ge(values_out, 16)
                clean_masks(dve, 0)


        def finish_ask(dve, source, asked):
            dve.tensor_scalar(work[:, :, :], source, 0.0, None, ALU.min).then_inc(asked, 1)

        def elu_exp(act, c):
            hold(act, elu_asked, c + 1)
            act.activation(work[:, :, :], work[:, :, :], ACT.Exp).then_inc(elu_given, 1)

        FIN = 9

        def finish_rows(dve, source, c, given_count, base):
            rows = bass.ds(c * CT, CT) if not isinstance(c, int) else slice(c * CT, (c + 1) * CT)
            flat = lambda ap: ap.rearrange("p t f -> p (t f)")
            dve.wait_ge(elu_given, given_count)
            dve.scalar_tensor_tensor(out=flat(work[:, :, :]), in0=flat(source), scalar=0.0, in1=flat(work[:, :, :]),
                                     op0=ALU.max, op1=ALU.add).then_inc(fin, 1)
            dve.wait_ge(fin, base + 1)
            dve.scalar_tensor_tensor(out=flat(work[:, :, :]), in0=flat(work[:, :, :]), scalar=-1.0,
                                     in1=flat(feat[:, rows, :]), op0=ALU.add, op1=ALU.add).then_inc(fin, 1)
            dve.wait_ge(fin, base + 2)
            for t in range(CT):
                last = dve.bn_stats(stats[:, t, 0:6], work[:, t, :])
            last.then_inc(fin, 1)
            hold(dve, fin, base + 3)
            for t in range(CT):
                last = dve.bn_aggr(mean_var[:, t, :], stats[:, t, 0:6])
            last.then_inc(fin, 1)
            dve.wait_ge(fin, base + 4)
            dve.tensor_copy(var[:, rows], mean_var[:, :, 1])
            dve.tensor_tensor(feat[:, rows, :], work[:, :, :], mean_var[:, :, 0:1].broadcast_to([P, CT, F]), ALU.subtract)\
                .then_inc(fin, 1)
            dve.wait_ge(fin, base + 5)
            for k in range(2):
                a = a1_spread[:, k:k + 1, :].broadcast_to([P, CT, F])
                dve.tensor_tensor(work[:, :, :], feat[:, rows, :], a, ALU.mult).then_inc(fin, 1)
                dve.wait_ge(fin, base + 6 + 2 * k)
                dve.reduce_sum(dots[:, k, rows], work[:, :, :], axis=AXX).then_inc(fin, 1)
                dve.wait_ge(fin, base + 7 + 2 * k)

        def slot_halves(u):
            s = u % SLOTS
            return ring[:, s, 0, :], ring[:, s, 1, :]

        def act_count(u):
            return sum(ON_ACT[k % UH] for k in range(u))

        def wait_s(engine, c, u):
            h = u // UH
            hold(engine, s_in[h % 2], c * 32 + 16 * (h // 2 + 1))

        def act_unit(act, c, u):
            h, g = divmod(u, UH)
            if g == 0:
                wait_s(act, c, u)
            if not ON_ACT[g]:
                return
            hold(act, unit_done, c * U + (u + 1))
            below = slot_halves(u)[1]
            for k in range(JU):
                j = g * JU + k
                last = act.activation(below[:, k * C:(k + 1) * C], s_rows[:, h % 2, :], ACT.Sign,
                                      bias=scores[:, j, h:h + 1], saturate=False)
                if k == JU - 1:
                    last.then_inc(signs_ready, 1)
            if g == UH - 1:
                act.wait_ge(signs_ready, c * NA + act_count(u + 1))
                act.sem_inc(s_read_act, 1)

        def dve_compare(dve, c, u):
            h, g = divmod(u, UH)
            hold(dve, unit_done, c * U + (u + 1))
            below = slot_halves(u)[1].bitcast(U8)
            for k in range(JU):
                j = g * JU + k
                last = dve.tensor_scalar(below[:, k * C:(k + 1) * C], s_rows[:, h % 2, :], neg_d[:, h, j:j + 1],
                                         float(TWO), ALU.is_lt, ALU.mult)
            last.then_inc(compared, 1)

        def dve_unit(dve, c, u):
            h, g = divmod(u, UH)
            if g == 0:
                wait_s(dve, c, u)
            if g + 1 < UH and not ON_ACT[g + 1]:
                dve_compare(dve, c, u + 1)
            above, below = (half.bitcast(I32) for half in slot_halves(u))
            m = masks[:, :].bitcast(I32)[:, g * (JU * C // 4):(g + 1) * (JU * C // 4)]
            if ON_ACT[g]:
                dve.wait_ge(signs_ready, c * NA + act_count(u + 1))
                dve.scalar_tensor_tensor(out=below, in0=below, scalar=1, in1=m, op0=ALU.logical_shift_right,
                                         op1=ALU.bitwise_and).then_inc(below_ready, 1)
            else:
                dve.wait_ge(compared, c * ND + (u + 1 - act_count(u + 1)))
                dve.tensor_tensor(below, below, m, ALU.bitwise_and).then_inc(below_ready, 1)
                if g == max(k for k in range(UH) if not ON_ACT[k]):
                    dve.sem_inc(s_read_dve, 1)
            dve.wait_ge(below_ready, c * U + (u + 1))
            dve.tensor_tensor(above, m, below, ALU.bitwise_xor).then_inc(unit_ready, 1)

        ev_done = sem("ev_done")

        def take_head(dve, c, h):
            for b in range(CT // 2):
                dve.wait_ge(acc_ready, c * (H * NB) + (h * NB + b + 1))
                parts = bank[b][:, 0:2 * W0].rearrange("p (m q k) -> p m k q", q=PARTS, k=K0)
                dve.tensor_reduce(evac[:, 2 * b:2 * b + 2, :, :].rearrange("p t b k -> p (t b) k"), parts, axis=AXX,
                                  op=ALU.add).then_inc(acc_taken, 1)
            dve.wait_ge(acc_taken, c * (H * NB) + ((h + 1) * NB + NB))
            rows = bass.ds(c * CT, CT) if not isinstance(c, int) else slice(c * CT, (c + 1) * CT)
            weigh(dve, ev_done, c * (WEIGH * H) + WEIGH * h, evac, mixed, empty, inverse, factors[:, h, rows, :],
                  mean_values[:, h * D:(h + 1) * D], D, CT, attended[:, :, h * D:(h + 1) * D])

        def pe_chunk(pe, c, build):
            for u in range(U):
                h, g = divmod(u, UH)
                if build:
                    for q in groups_at(u):
                        turn_group(pe, c + 1, q)
                hold(pe, unit_ready, c * U + (u + 1))
                above, below = slot_halves(u)
                for t in range(CT):
                    b, at = t // 2, (t % 2) * W0
                    if g == 0 and t % 2 == 0:
                        hold(pe, acc_taken, c * (H * NB) + (h * NB + b + 1))
                    for k in range(JU):
                        j = g * JU + k
                        for side, half in enumerate((above, below)):
                            first = j == 0 and t % 2 == 0 and side == 0
                            lo = at + side * PARTS * K0
                            last = pe.matmul(bank[b][:, lo:lo + PARTS * K0],
                                             half[:, k * C + t * P:k * C + (t + 1) * P],
                                             moving[:, j, h, side * PARTS * K0:(side + 1) * PARTS * K0],
                                             start=first, stop=(j == T - 1), skip_group_check=True)
                    if g == UH - 1 and t % 2 == 1:
                        last.then_inc(acc_ready, 1)
                    elif t == CT - 1:
                        last.then_inc(unit_done, 1)
                if g == UH - 1:
                    pe.wait_ge(acc_ready, c * (H * NB) + (h + 1) * NB)
                    pe.sem_inc(unit_done, 1)

        def only_if(engine, flag_ap, wanted):
            value = engine.value_load(flag_ap, min_val=0, max_val=1)
            return engine.If(value > 0 if wanted else value < 1)

        with nc.Block() as block:
            @block.gpsimd
            def _(pool):
                with only_if(pool, flag[0:1, 0:1], False):
                    with pool.Fori(0, NC - 1) as c:
                        for t in range(CT):
                            pool.wait_ge(turned, c * Q + (Q + (t - 1) * QT))
                            load_adj(pool, c + 1, t)

            @block.sync
            def _(sp):
                with only_if(sp, flag[0:1, 0:1], False):
                    def keep(c):
                        sp.wait_ge(mask_ready, c + 1)
                        dst = masks_kept[bass.ds(c, 1), :, :, :] if not isinstance(c, int) else masks_kept[c:c + 1, :, :, :]
                        sp.dma_start(dst.rearrange("o p t i -> (o p) (t i)"), masks[:, :].bitcast(I32)).then_inc(kept, 16)

                    def load_s(c, h, before):
                        sp.wait_ge(s_read_act, before)
                        sp.wait_ge(s_read_dve, before)
                        cols = bass.ds(c * C, C) if not isinstance(c, int) else slice(c * C, (c + 1) * C)
                        sp.dma_start(s_rows[:, h % 2, :], score_rows[H + h:H + h + 1, cols].broadcast_to([P, C]))\
                            .then_inc(s_in[h % 2], 16)

                    with sp.Fori(0, NC - 1) as c:
                        keep(c)
                        load_s(c, 2, c * H + 1)
                        load_s(c, 3, c * H + 2)
                        load_s(c + 1, 0, c * H + 3)
                        load_s(c + 1, 1, c * H + 4)
                    keep(NC - 1)
                    load_s(NC - 1, 2, (NC - 1) * H + 1)
                    load_s(NC - 1, 3, (NC - 1) * H + 2)
                    sp.wait_ge(kept, 16 * NC)

            @block.tensor
            def _(pe):
                with only_if(pe, flag[0:1, 0:1], False):
                    pe.sem_inc(unit_done, SLOTS)
                    pe.sem_inc(acc_taken, NB)
                    with pe.Fori(0, NC - 1) as c:
                        pe_chunk(pe, c, True)
                    pe_chunk(pe, NC - 1, False)

            @block.scalar
            def _(act):
                with only_if(act, flag[0:1, 0:1], False):
                    def part(c, units, build):
                        for u in units:
                            act_unit(act, c, u)
                            if build:
                                for q in groups_at(u - LAG):
                                    if q == 0:
                                        hold(act, mask_ready, c + 1)
                                    take_group(act, c + 1, q)

                    part(0, range(ROT), False)
                    with act.Fori(0, NC - 1) as c:
                        part(c, range(ROT, U), True)
                        part(c + 1, range(6), False)
                        elu_exp(act, c)
                        part(c + 1, range(6, ROT), False)
                    part(NC - 1, range(ROT, U), False)
                    elu_exp(act, NC - 1)

            @block.vector
            def _(dve):
                with only_if(dve, flag[0:1, 0:1], False):
                    def units(c, which):
                        for u in which:
                            dve_unit(dve, c, u)
                            for h in range(H - 1):
                                if u == UH * (h + 1) + 1:
                                    take_head(dve, c, h)

                    def close(c):
                        take_head(dve, c, H - 1)
                        dve.wait_ge(ev_done, c * (WEIGH * H) + WEIGH * H)
                        finish_ask(dve, attended[:, :, :], elu_asked)

                    dve.wait_ge(mask_ready, 1)
                    units(0, range(ROT))
                    with dve.Fori(0, NC - 1) as c:
                        units(c, range(ROT, U))
                        hold(dve, kept, c * 16 + 16)
                        dve.wait_ge(unit_ready, c * U + U)
                        clean_masks(dve, c + 1)
                        dve.wait_ge(mask_ready, c + 2)
                        units(c + 1, range(2))
                        close(c)
                        units(c + 1, range(2, ROT))
                        finish_rows(dve, attended[:, :, :], c, c + 1, c * FIN)
                    units(NC - 1, range(ROT, U))
                    close(NC - 1)
                    finish_rows(dve, attended[:, :, :], NC - 1, NC, (NC - 1) * FIN)

        fast0.close()

        general0 = ExitStack()
        summed = sb("summed", [P, T, F], F32, general0)

        def finish0(dve, act):
            for c in range(NC):
                if dve is not None:
                    source = summed[:, c * CT:(c + 1) * CT, :]
                    finish_ask(dve, source, elu_asked)
                    finish_rows(dve, source, c, c + 1, c * FIN)
                else:
                    elu_exp(act, c)

        general_attention(0, H, D, flag[0:1, 0:1], score_rows[0:H, :],
                          lambda it, h: one(scores[:, bass.ds(it, 1), H + h:H + h + 1]), None, summed, finish0)
        general0.close()

        moving1 = sb("moving1", [P, T, 2 * PARTS * K1], BF16)
        values1 = sb("values1", [P, T, F])
        scores1 = sb("scores1", [P, T, 2])
        inv_std = sb("inv_std", [P, T])
        rows = sb("rows", [P, 12, T])
        turned_scores1 = sb("turned_scores1", [T, 2, P])
        factors1 = sb("factors1", [P, 1, T, 2])
        above_d1, below_d1, neg_d1 = (sb(n, [P, 1, T]) for n in ("above_d1", "below_d1", "neg_d1"))
        seen1, column1, low1, centre1 = sb("seen1", [P, 8]), sb("column1", [P, 1]), sb("low1", [P, 1]), sb("centre1", [P, 1])
        ones1 = sb("ones1", [P, P])
        mean_values1 = sb("mean_values1", [P, F])
        work1 = sb("work1", [P, RT, F])
        result = sb("result", [P, 2, RT, F])
        small = sb("small", [P, 8, RT])
        stats1 = sb("stats1", [P, RT, 8])
        mean_var1 = sb("mean_var1", [P, RT, 2])
        fast1 = ExitStack()
        pair = sb("pair", [P, 2, 2, T * R], FP8, fast1)
        s_rows1 = sb("s_rows1", [P, 2, R], F32, fast1)
        GT = 8
        NG = T // GT
        part_b1, part_d1 = (sb(n, [P, GT, K1], F32, fast1) for n in ("part_b1", "part_d1"))

        roots_asked, roots_given, logs_asked, logs_given, dve1 = sems(
            "roots_asked", "roots_given", "logs_asked", "logs_given", "dve1")
        scores1_ready, scores1_turned, scores1_copied, scores1_out = sems(
            "scores1_ready", "scores1_turned", "scores1_copied", "scores1_out")
        values1_ready, mean1_ready, ones1_ready, exp1_asked, exp1_given = sems(
            "values1_ready", "mean1_ready", "ones1_ready", "exp1_asked", "exp1_given")
        extrema1_ready, extrema1_turned, extrema1_given = sems("extrema1_ready", "extrema1_turned", "extrema1_given")
        mask_in = sems("mask_in0", "mask_in1")
        s_run_in = sems("s_run_in0", "s_run_in1")

        def over(ap, tiles, width):
            return ap.rearrange("p (t o) -> p t o", o=1).broadcast_to([P, tiles, width])

        def load_run(sp, e, y):
            per = C // R
            words = slice((y % per) * R // 4, (y % per + 1) * R // 4)
            src = masks_kept[bass.ds(e // per, 1), :, :, words] if not isinstance(e, int) else \
                masks_kept[e // per:e // per + 1, :, :, words]
            sp.dma_start(pair[:, y, 0, :].bitcast(I32).rearrange("p (t i) -> p t i", i=R // 4),
                         src.rearrange("o p t i -> (o p) t i"))\
                .then_inc(mask_in[y], 16)
            cols = slice(e * R, (e + 1) * R) if isinstance(e, int) else bass.ds(e * R, R)
            sp.dma_start(s_rows1[:, y, :], score_rows1[1:2, cols].broadcast_to([P, R])).then_inc(s_run_in[y], 16)

        with nc.Block() as block:
            @block.gpsimd
            def _(pool):
                pool.memset(ones1[:, :], 1.0).then_inc(ones1_ready, 1)

            @block.sync
            def _(sp):
                sp.wait_ge(scores1_copied, 1)
                sp.dma_start(score_rows1.rearrange("k (t p) -> t k p", p=P), turned_scores1[:, :, :]).then_inc(scores1_out, 16)
                sp.wait_ge(scores1_out, 16)

            @block.scalar
            def _(act):
                act.wait_ge(roots_asked, 1)
                act.activation(rows[:, 2:4, :], rows[:, 0:2, :], ACT.Sqrt).then_inc(roots_given, 1)
                act.wait_ge(logs_asked, 1)
                act.activation(rows[:, 8:10, :], rows[:, 8:10, :], ACT.Ln).then_inc(logs_given, 1)
                act.wait_ge(scores1_turned, 1)
                act.activation(turned_scores1[:, :, :].rearrange("t k p -> t (k p)"), bank[0][0:T, 0:2 * P], ACT.Copy)\
                    .then_inc(scores1_copied, 1)
                act.wait_ge(exp1_asked, 1)
                act.activation(above_d1[:, :, :], above_d1[:, :, :], ACT.Exp).then_inc(exp1_given, 1)
                act.activation(below_d1[:, :, :], below_d1[:, :, :], ACT.Exp).then_inc(exp1_given, 1)
                act.activation(factors1[:, :, :, :], factors1[:, :, :, :], ACT.Exp).then_inc(exp1_given, 1)

            @block.tensor
            def _(pe):
                pe.wait_ge(scores1_ready, 1)
                for k in range(2):
                    last = pe.transpose(bank[0][0:T, k * P:(k + 1) * P], scores1[:, :, k], ident[:, :])
                last.then_inc(scores1_turned, 1)
                pe.wait_ge(ones1_ready, 1)
                pe.wait_ge(extrema1_ready, 1)
                pe.transpose(bank[3][0:6, 0:P], seen1[:, 0:6], ident[:, :]).then_inc(extrema1_turned, 1)
                pe.wait_ge(extrema1_given, 1)
                pe.matmul(bank[3][:, P:P + 6], ones1[0:6, :], seen1[0:6, 0:6], start=True, stop=True)\
                    .then_inc(extrema1_turned, 1)
                pe.wait_ge(values1_ready, 1)
                for t in range(T):
                    last = pe.matmul(bank[2][:, 0:F], ones1[:, :], values1[:, t, :], start=(t == 0), stop=(t == T - 1))
                last.then_inc(mean1_ready, 1)

            @block.vector
            def _(dve):
                step = Chain(dve, dve1)
                step(dve.tensor_scalar(rows[:, 0, :], var[:, :], LN_EPS, None, ALU.add))
                dve.tensor_scalar(rows[:, 1, :], var[:, :], float(F), None, ALU.mult).then_inc(roots_asked, 1)
                dve.wait_ge(roots_given, 1)
                newton_root(step, rows[:, 2:4, :], rows[:, 0:2, :], rows[:, 4:6, :])
                norm, square, scratch, ratio, near = (rows[:, k, :] for k in (6, 7, 10, 11, 5))
                plus, minus = rows[:, 8, :], rows[:, 9, :]
                step(dve.reciprocal(inv_std[:, :], rows[:, 2, :]))
                step(dve.tensor_tensor(norm, rows[:, 3, :], inv_std[:, :], ALU.mult))
                step(dve.tensor_scalar(norm, norm, EPS, 1.0 - EPS, ALU.max, ALU.min))
                dve.tensor_scalar(plus, norm, 1.0, None, ALU.add)
                dve.tensor_scalar(minus, norm, -1.0, 1.0, ALU.mult, ALU.add).then_inc(logs_asked, 1)
                step(dve.reciprocal(scratch, norm))
                step(dve.tensor_tensor(square, norm, norm, ALU.mult))
                step(dve.tensor_scalar(near, square, 1.0 / 9, 1.0 / 7, ALU.mult, ALU.add))
                for c in (5, 3, 1):
                    step(dve.tensor_tensor(near, near, square, ALU.mult))
                    step(dve.tensor_scalar(near, near, 1.0 / c, None, ALU.add))
                step(dve.tensor_scalar(square, norm, 0.1, None, ALU.is_lt))
                dve.wait_ge(logs_given, 1)
                step(dve.tensor_tensor(ratio, plus, minus, ALU.subtract))
                step(dve.tensor_tensor(ratio, ratio, scratch, ALU.mult))
                step(dve.tensor_scalar(ratio, ratio, 0.5, None, ALU.mult))
                step(dve.tensor_tensor(near, near, ratio, ALU.subtract))
                step(dve.tensor_tensor(near, near, square, ALU.mult))
                step(dve.tensor_tensor(ratio, ratio, near, ALU.add))
                step(dve.tensor_tensor(ratio, ratio, inv_std[:, :], ALU.mult))
                dve.tensor_tensor(scores1[:, :, 0], dots[:, 1, :], ratio, ALU.mult)
                dve.tensor_tensor(scores1[:, :, 1], dots[:, 0, :], ratio, ALU.mult).then_inc(scores1_ready, 1)
                dve.wait_ge(scores1_ready, 1)
                by_kind = scores1[:, :, :].rearrange("p t k -> p k t")
                step(dve.memset(seen1[:, :], 0.0))
                dve.tensor_reduce(seen1[:, 0:2], by_kind, axis=AXX, op=ALU.max)
                step(dve.tensor_reduce(seen1[:, 2:4], by_kind, axis=AXX, op=ALU.min))
                dve.tensor_scalar(seen1[:, 2:4], seen1[:, 2:4], -1.0, None, ALU.mult).then_inc(extrema1_ready, 1)
                dve.tensor_tensor(values1[:, :, :], feat[:, :, :], over(ratio, T, F), ALU.mult).then_inc(values1_ready, 1)
                bounds(step, 1, seen1, column1, bank[3], low1[:, :], centre1[:, :], flag1, extrema1_turned, extrema1_given)
                step(dve.tensor_tensor(flag1[0:1, 0:1], flag1[0:1, 0:1], flag[0:1, 0:1], ALU.max))
                exponents(step, exp1_asked, 1, lambda h: scores1[:, :, 0], lambda h: scores1[:, :, 1],
                          low1[:, :], centre1[:, :], above_d1, below_d1, factors1, neg_d1)
                dve.wait_ge(mean1_ready, 1)
                step(dve.tensor_scalar(mean_values1[:, :], bank[2][:, 0:F], 1.0 / N, None, ALU.mult))

        evac1 = sb("evac1", [P, RT, 2, K1], F32, fast1)
        mixed1 = sb("mixed1", [P, RT, K1], F32, fast1)
        empty1 = sb("empty1", [P, RT, F], F32, fast1)
        inverse1 = sb("inverse1", [P, 2, RT], F32, fast1)
        attended1 = sb("attended1", [P, RT, F], F32, fast1)
        signs1_ready, compared1, below1_ready, group_ready, tile_ready, pair_taken = sems(
            "signs1_ready", "compared1", "below1_ready", "group_ready", "tile_ready", "pair_taken")
        norm_done, close_done, func_asked, func_given, result_ready = sems(
            "norm_done", "close_done", "func_asked", "func_given", "result_ready")
        stored = sems("stored_even", "stored_odd")
        POOL_GROUPS = 1
        HALF = GT // 2

        def run_rows(e):
            return slice(e * RT, (e + 1) * RT) if isinstance(e, int) else bass.ds(e * RT, RT)

        dve2, pool1, below_weighed, moving1_ready = sems("dve2", "pool1", "below_weighed", "moving1_ready")

        def weigh_group(step, g, b, part, weight):
            js = slice(g * GT, (g + 1) * GT)
            weight = weight[:, 0, js]
            step(step.engine.tensor_tensor(part[:, :, 0:F], values1[:, js, :], over(weight, GT, F), ALU.mult))
            step(step.engine.tensor_copy(part[:, :, F:K1], weight.rearrange("p (t o) -> p t o", o=1)))
            split(step, part[:, :, :], *(moving1[:, js, (b * PARTS + q) * K1:(b * PARTS + q + 1) * K1]
                                         for q in range(PARTS)))

        CLOSE = 29

        def close_run(dve, v, e, y):
            step = Chain(dve, close_done, e * CLOSE)
            raw2, raw, scratch, norm, gain, big, root = (small[:, k, :] for k in range(7))
            step(dve.tensor_tensor(work1[:, :, :], v, v, ALU.mult))
            step(dve.reduce_sum(raw2, work1[:, :, :], axis=AXX))
            dve.tensor_copy(norm, raw2).then_inc(func_asked, 1)
            dve.wait_ge(func_given, e * 3 + 1)
            newton_root(step, raw, raw2, scratch)
            step(dve.tensor_scalar(norm, raw, EPS, None, ALU.max))
            dve.tensor_copy(scratch, norm).then_inc(func_asked, 1)
            dve.wait_ge(func_given, e * 3 + 2)
            step(dve.reciprocal(scratch, norm))
            step(dve.tensor_tensor(gain, gain, scratch, ALU.mult))
            step(dve.tensor_tensor(norm, gain, raw, ALU.mult))
            step(dve.tensor_scalar(norm, norm, EPS, None, ALU.max))
            step(dve.tensor_scalar(big, norm, MAX_NORM, None, ALU.is_gt))
            step(dve.reciprocal(scratch, norm))
            step(dve.tensor_scalar(scratch, scratch, MAX_NORM, -1.0, ALU.mult, ALU.add))
            step(dve.tensor_tensor(scratch, scratch, big, ALU.mult))
            step(dve.tensor_scalar(scratch, scratch, 1.0, None, ALU.add))
            step(dve.tensor_tensor(gain, gain, scratch, ALU.mult))
            dve.wait_ge(stored[y], (e - y) * 8 + 16)
            step(dve.tensor_tensor(work1[:, :, :], v, over(gain, RT, F), ALU.mult))
            step(dve.tensor_tensor(result[:, y, :, :], feat[:, run_rows(e), :], over(inv_std[:, run_rows(e)], RT, F), ALU.mult))
            step(dve.tensor_tensor(result[:, y, :, :], result[:, y, :, :], work1[:, :, :], ALU.add))
            for t in range(RT):
                last = dve.bn_stats(stats1[:, t, 0:6], result[:, y, t, :])
            step(last)
            if not isinstance(e, int):
                dve.sem_inc(passed, 1)
            for t in range(RT):
                last = dve.bn_aggr(mean_var1[:, t, :], stats1[:, t, 0:6])
            step(last)
            dve.tensor_scalar(raw2, mean_var1[:, :, 1], LN_EPS, None, ALU.add).then_inc(func_asked, 1)
            dve.wait_ge(func_given, e * 3 + 3)
            newton_root(step, root, raw2, scratch)
            step(dve.reciprocal(root, root))
            for t in range(RT):
                last = dve.tensor_scalar(result[:, y, t, :], result[:, y, t, :], mean_var1[:, t, 0:1], root[:, t:t + 1],
                                         ALU.subtract, ALU.mult)
            last.then_inc(result_ready, 1)
            assert step.count == CLOSE, step.count

        def free_results(act):
            for y in range(2):
                act.sem_inc(stored[y], 16)

        def wait_results(act):
            for y in range(2):
                act.wait_ge(stored[y], 16 + 8 * NR)

        def close_act(act, e, y):
            raw2, raw, scratch, norm, gain, big, root = (small[:, k, :] for k in range(7))
            for n, (to, frm, func) in enumerate(((raw, norm, ACT.Sqrt), (gain, scratch, ACT.Tanh), (root, raw2, ACT.Sqrt))):
                act.wait_ge(func_asked, e * 3 + (n + 1))
                act.activation(to, frm, func).then_inc(func_given, 1)
            act.wait_ge(result_ready, e + 1)
            act.dma_start(out_rows[:, run_rows(e), :], result[:, y, :, :]).then_inc(stored[y], 16)

        with nc.Block() as block:
            @block.gpsimd
            def _(pool):
                with only_if(pool, flag1[0:1, 0:1], False):
                    step = Chain(pool, pool1)
                    for g in range(NG - POOL_GROUPS, NG):
                        weigh_group(step, g, 1, part_d1, below_d1)
                        pool.sem_inc(below_weighed, 1)

            @block.sync
            def _(sp):
                with only_if(sp, flag1[0:1, 0:1], False):
                    load_run(sp, 0, 0)
                    load_run(sp, 1, 1)
                    with sp.Fori(0, NR // 2 - 1) as n:
                        for y in range(2):
                            sp.wait_ge(tile_ready, n * (2 * RT) + RT * (y + 1))
                            load_run(sp, n * 2 + (2 + y), y)

            @block.scalar
            def _(act):
                with only_if(act, flag1[0:1, 0:1], False):
                    free_results(act)

                    def signs(e, y):
                        hold(act, s_run_in[y], (e - y) * 8 + 16)
                        for g in range(NG):
                            for k in range(HALF):
                                j = g * GT + k
                                last = act.activation(pair[:, y, 1, j * R:(j + 1) * R], s_rows1[:, y, :], ACT.Sign,
                                                      bias=scores1[:, j, 0:1], saturate=False)
                            last.then_inc(signs1_ready, 1)

                    signs(0, 0)
                    signs(1, 1)
                    with act.Fori(0, NR // 2 - 1) as n:
                        for y in range(2):
                            close_act(act, n * 2 + y, y)
                            hold(act, tile_ready, n * (2 * RT) + RT * (y + 1))
                            signs(n * 2 + (2 + y), y)
                    for y in range(2):
                        close_act(act, NR - 2 + y, y)
                    wait_results(act)

            @block.tensor
            def _(pe):
                with only_if(pe, flag1[0:1, 0:1], False):
                    pe.sem_inc(pair_taken, RT)

                    def run(e, y):
                        for t in range(RT):
                            hold(pe, pair_taken, e * RT + (t + 1))
                            for j in range(T):
                                if t == 0 and j % GT == 0:
                                    hold(pe, group_ready, e * NG + (j // GT + 1))
                                for side in range(2):
                                    last = pe.matmul(bank[2 * t + side][:, 0:PARTS * K1],
                                                     pair[:, y, side, j * R + t * P:j * R + (t + 1) * P],
                                                     moving1[:, j, side * PARTS * K1:(side + 1) * PARTS * K1],
                                                     start=(j == 0), stop=(j == T - 1))
                            last.then_inc(tile_ready, 1)

                    def first_run():
                        pe.wait_ge(pair_taken, RT)
                        for j in range(T):
                            if j % GT == 0:
                                pe.wait_ge(group_ready, j // GT + 1)
                                pe.wait_ge(moving1_ready, j // GT + 1)
                                if j // GT >= NG - POOL_GROUPS:
                                    pe.wait_ge(below_weighed, j // GT - (NG - POOL_GROUPS) + 1)
                            for t in range(RT):
                                for side in range(2):
                                    last = pe.matmul(bank[2 * t + side][:, 0:PARTS * K1],
                                                     pair[:, 0, side, j * R + t * P:j * R + (t + 1) * P],
                                                     moving1[:, j, side * PARTS * K1:(side + 1) * PARTS * K1],
                                                     start=(j == 0), stop=(j == T - 1))
                                if j == T - 1:
                                    last.then_inc(tile_ready, 1)

                    first_run()
                    run(1, 1)
                    with pe.Fori(1, NR // 2) as n:
                        for y in range(2):
                            run(n * 2 + y, y)

            @block.vector
            def _(dve):
                with only_if(dve, flag1[0:1, 0:1], False):
                    step = Chain(dve, dve2)

                    def split_masks(e, y, weigh_too=False):
                        hold(dve, mask_in[y], (e - y) * 8 + 16)
                        hold(dve, s_run_in[y], (e - y) * 8 + 16)
                        s = s_rows1[:, y, :]
                        above, below = (pair[:, y, k, :] for k in range(2))
                        w = lambda ap, lo, n: ap.bitcast(I32)[:, lo * R // 4:(lo + n) * R // 4]
                        for g in range(NG):
                            for k in range(HALF, GT):
                                j = g * GT + k
                                last = dve.tensor_scalar(below[:, j * R:(j + 1) * R].bitcast(U8), s, neg_d1[:, 0, j:j + 1],
                                                         float(TWO), ALU.is_lt, ALU.mult)
                            last.then_inc(compared1, 1)
                            dve.wait_ge(signs1_ready, e * NG + (g + 1))
                            signs, here = w(below, g * GT, HALF), w(above, g * GT, HALF)
                            dve.scalar_tensor_tensor(out=signs, in0=signs, scalar=1, in1=here,
                                                     op0=ALU.logical_shift_right, op1=ALU.bitwise_and)
                            dve.wait_ge(compared1, e * NG + (g + 1))
                            mine, here = w(below, g * GT + HALF, HALF), w(above, g * GT + HALF, HALF)
                            dve.tensor_tensor(mine, mine, here, ALU.bitwise_and).then_inc(below1_ready, 1)
                            dve.wait_ge(below1_ready, e * NG + (g + 1))
                            dve.tensor_tensor(w(above, g * GT, GT), w(above, g * GT, GT), w(below, g * GT, GT),
                                              ALU.bitwise_xor).then_inc(group_ready, 1)
                            if weigh_too:
                                weigh_group(step, g, 0, part_b1, above_d1)
                                if g < NG - POOL_GROUPS:
                                    weigh_group(step, g, 1, part_b1, below_d1)
                                dve.sem_inc(moving1_ready, 1)

                    def take_run(e, y):
                        for t in range(RT):
                            dve.wait_ge(tile_ready, e * RT + (t + 1))
                            for side in range(2):
                                parts = bank[2 * t + side][:, 0:PARTS * K1].rearrange("p (q k) -> p k q", q=PARTS)
                                last = dve.tensor_reduce(evac1[:, t, side, :], parts, axis=AXX, op=ALU.add)
                            last.then_inc(pair_taken, 1)
                        dve.wait_ge(pair_taken, e * RT + 2 * RT)
                        weigh(dve, norm_done, e * WEIGH, evac1, mixed1, empty1, inverse1, factors1[:, 0, run_rows(e), :],
                              mean_values1[:, :], F, RT, attended1[:, :, :])
                        close_run(dve, attended1[:, :, :], e, y)

                    split_masks(0, 0, weigh_too=True)
                    split_masks(1, 1)
                    with dve.Fori(0, NR // 2 - 1) as n:
                        for y in range(2):
                            take_run(n * 2 + y, y)
                            split_masks(n * 2 + (2 + y), y)
                    for y in range(2):
                        take_run(NR - 2 + y, y)

        fast1.close()

        def finish1(dve, act):
            if act is not None:
                free_results(act)
            for e in range(NR):
                if dve is not None:
                    close_run(dve, summed1[:, e * RT:(e + 1) * RT, :], e, e % 2)
                else:
                    close_act(act, e, e % 2)
            if act is not None:
                wait_results(act)

        summed1 = sb("summed1", [P, T, F])
        general_attention(1, 1, F, flag1[0:1, 0:1], score_rows1[0:1, :],
                          lambda it, h: one(scores1[:, bass.ds(it, 1), 1:2]), values1, summed1, finish1)


_INS = ['x', 'adj', 'L0_gnn_W', 'L0_gnn_a', 'L1_gnn_a']
_OUTS = [((4096, 128), 'float32')]


def kernel(**inputs):
    import numpy as _np
    import concourse.bacc as _bacc
    from concourse import mybir as _mybir
    from concourse.bass_utils import run_bass_kernel_spmd as _run

    nc = _bacc.Bacc("TRN2", target_bir_lowering=False, num_devices=1)
    arrays, args = {}, []
    for name in _INS:
        a = _np.ascontiguousarray(inputs[name])
        arrays[f"in_{name}_dram"] = a
        args.append(nc.dram_tensor(f"in_{name}_dram", a.shape, _mybir.dt.from_np(a.dtype), kind="ExternalInput").ap())
    for i, (shape, dtype) in enumerate(_OUTS):
        dt = _mybir.dt.from_np(_np.dtype(dtype))
        args.append(nc.dram_tensor(f"out_{i}_dram", shape, dt, kind="ExternalOutput").ap())
    two_layer_gat(nc, *args)
    r = _run(nc, [arrays], core_ids=[0])
    return r.results[0]["out_0_dram"]
```

```python
import concourse.bass as bass
from concourse import mybir
from contextlib import ExitStack


F32, BF16, FP8, I32, U8 = (mybir.dt.float32, mybir.dt.bfloat16, mybir.dt.float8e4, mybir.dt.int32, mybir.dt.uint8)
ALU = mybir.AluOpType
ACT = mybir.ActivationFunctionType
AXX = mybir.AxisListType.X

P = 128
SLOPE = 0.2
NEG_INF = 9.0e15
EPS = 1e-7
MAX_NORM = 1.0 - 0.001
LN_EPS = 1e-5
BANK = 512
PARTS = 3
TWO = 0x40
TWOS = 0x40404040
SIGNS = 0x80808080 - (1 << 32)

WIDEST = 150.0
WIDEST_ALL = 154.0
LARGEST_SCORE = 300.0
LARGEST_VALUE = 90.0
LARGEST_EXPONENT = 80.0


class Chain:

    def __init__(self, engine, semaphore, before=0):
        self.engine, self.semaphore, self.before, self.count = engine, semaphore, before, 0

    def __call__(self, instruction):
        self.count += 1
        instruction.then_inc(self.semaphore, 1)
        self.engine.wait_ge(self.semaphore, self.before + self.count)


def two_layer_gat(nc, x, adj, W, a0, a1, out):
    N, F = x.shape
    H, D = a0.shape[1], a0.shape[2] // 2
    T = N // P
    x_rows = x.rearrange("(t p) f -> p t f", p=P)
    out_rows = out.rearrange("(t p) f -> p t f", p=P)

    CT = 8
    C = CT * P
    NC = T // CT
    JU = 4
    UH = T // JU
    U = H * UH
    NB = CT // 2
    SLOTS = 4
    K0 = D + 1
    K1 = F + 1
    W0 = 2 * PARTS * K0
    ON_ACT = [who == "A" for who in H * "AVAVAAVA"]
    NA, ND = sum(ON_ACT), U - sum(ON_ACT)
    DIRECT = [how == "D" for how in H * "DD-D----"]
    GQ = 8
    QT = T // GQ
    Q = CT * QT
    FIRST_STEP, LAST_STEP = 6, 27
    ROT, DVE_ROT = 8, 16
    CLOSE_AT = 1
    PIECES_AT = [3, 4, 5, 6, 11, 13]
    EARLY = QT
    ACT_GROUPS = 3
    ON_POOL = 1
    LAG = 3

    def groups_at(u):
        if not FIRST_STEP <= u <= LAST_STEP:
            return range(0)
        n = LAST_STEP - FIRST_STEP + 1
        k = u - FIRST_STEP
        return range(k * Q // n, (k + 1) * Q // n)

    RT = 4
    R = RT * P
    NR = T // RT

    score_rows = nc.dram_tensor("score_rows", (2 * H, N), F32, kind="Internal").ap()
    score_rows1 = nc.dram_tensor("score_rows1", (2, N), F32, kind="Internal").ap()
    values_kept = nc.dram_tensor("values_kept", (P, T, F), F32, kind="Internal").ap()
    masks_kept = nc.dram_tensor("masks_kept", (NC, P, T, C // 4), I32, kind="Internal").ap()

    ctx = ExitStack()
    with ctx:
        def sb(name, shape, dt=F32, where=ctx):
            return where.enter_context(nc.sbuf_tensor(name, shape, dt))

        def sem(name):
            return ctx.enter_context(nc.semaphore(name))

        def sems(*names):
            return [sem(n) for n in names]

        def hold(engine, semaphore, value):
            engine.wait_ge(semaphore, value)
            if not isinstance(value, int):
                engine.sem_inc(passed, 1)

        passed = sem("passed")

        def one(ap):
            return ap.rearrange("p a b -> p (a b)")

        ident = sb("ident", [P, P])
        feat = sb("feat", [P, T, F])
        a1_spread = sb("a1_spread", [P, 2, F])
        scores = sb("scores", [P, T, 2 * H])
        work = sb("work", [P, CT, F])
        stats = sb("stats", [P, CT, 8])
        mean_var = sb("mean_var", [P, CT, 2])
        var = sb("var", [P, T])
        dots = sb("dots", [P, 2, T])
        flag = sb("flag", [1, 1], I32)
        flag1 = sb("flag1", [1, 1], I32)
        factors = sb("factors", [P, H, T, 2])
        mean_values = sb("mean_values", [P, F])
        bank = [ctx.enter_context(nc.psum_tensor(f"bank{i}", [P, BANK], F32)) for i in range(8)]


        def bounds(step, H, seen, column, spread_bank, low, centre, flag_out, turned, given):
            e = step.engine
            e.wait_ge(turned, 1)
            step(e.reduce_max(column[0:4 * H + 2, :], spread_bank[0:4 * H + 2, 0:P], axis=AXX))
            e.tensor_scalar(seen[0:4 * H + 2, 0:4 * H + 2], ident[0:4 * H + 2, 0:4 * H + 2],
                            column[0:4 * H + 2, 0:1], None, ALU.mult).then_inc(given, 1)
            e.wait_ge(turned, 2)
            b = seen
            step(e.tensor_copy(b[:, 0:4 * H + 2], spread_bank[:, P:P + 4 * H + 2]))
            d_max, s_max, d_min, s_min = (b[:, k * H:(k + 1) * H] for k in range(4))
            step(e.tensor_tensor(low, d_min, s_max, ALU.min))
            step(e.tensor_scalar(centre, d_max, -1.0, None, ALU.mult))
            step(e.tensor_tensor(low, low, centre, ALU.max))
            step(e.tensor_tensor(centre, d_max, low, ALU.subtract))
            step(e.tensor_scalar(centre, centre, 0.5, None, ALU.mult))
            w = b[:, 4 * H + 2:5 * H + 2]
            w_all = b[:, 5 * H + 2:6 * H + 2]
            step(e.tensor_tensor(w, d_max, low, ALU.add))
            step(e.tensor_scalar(w, w, 1.0 / WIDEST, None, ALU.mult))
            step(e.tensor_tensor(w_all, d_max, d_min, ALU.add))
            step(e.tensor_scalar(w_all, w_all, 1.0 / WIDEST_ALL, None, ALU.mult))
            step(e.tensor_scalar(b[:, 0:4 * H], b[:, 0:4 * H], 1.0 / LARGEST_SCORE, None, ALU.mult))
            step(e.tensor_scalar(b[:, 4 * H:4 * H + 2], b[:, 4 * H:4 * H + 2], 1.0 / LARGEST_VALUE, None, ALU.mult))
            step(e.reduce_max(column[:, :], b[:, 0:6 * H + 2], axis=AXX))
            step(e.tensor_scalar(flag_out[0:1, 0:1], column[0:1, 0:1], 1.0, None, ALU.is_gt))
            step(e.tensor_scalar(low, low, -1.0, None, ALU.mult))

        def exponents(step, exp_asked, H, d_of, s_of, centre, up, down, rows, negative_d):
            e = step.engine
            for h in range(H):
                e.tensor_scalar(up[:, h, :], d_of(h), centre[:, h:h + 1], None, ALU.subtract)
                e.tensor_scalar(down[:, h, :], d_of(h), SLOPE, None, ALU.mult)
                e.tensor_scalar(negative_d[:, h, :], d_of(h), -1.0, None, ALU.mult)
                step(e.tensor_scalar(rows[:, h, :, 0], s_of(h), 1.0 - SLOPE, centre[:, h:h + 1], ALU.mult, ALU.add))
                step(e.tensor_scalar(rows[:, h, :, 1], rows[:, h, :, 0], -1.0, 0.0, ALU.mult, ALU.min))
                step(e.tensor_scalar(rows[:, h, :, 0], rows[:, h, :, 0], 0.0, None, ALU.min))
            e.tensor_scalar(up[:, :, :], up[:, :, :], LARGEST_EXPONENT, None, ALU.min)
            e.tensor_scalar(down[:, :, :], down[:, :, :], LARGEST_EXPONENT, None, ALU.min).then_inc(exp_asked, 1)

        def split(step, source, high, middle, lowest):
            e = step.engine
            step(e.tensor_copy(high, source))
            step(e.tensor_tensor(source, source, high, ALU.subtract))
            step(e.tensor_copy(middle, source))
            step(e.tensor_tensor(lowest, source, middle, ALU.subtract))

        def newton_root(step, root, square, scratch):
            e = step.engine
            step(e.tensor_scalar(root, root, 1e-30, None, ALU.max))
            step(e.reciprocal(scratch, root))
            step(e.tensor_tensor(scratch, scratch, square, ALU.mult))
            step(e.tensor_tensor(root, root, scratch, ALU.add))
            step(e.tensor_scalar(root, root, 0.5, None, ALU.mult))

        WEIGH = 7

        def weigh(dve, done, before, sides, mixed, empty, inverse, factors, mean, width, tiles, out):
            step = Chain(dve, done, before)
            flat = sides[:, :, :, :].rearrange("p t b k -> p (t b) k")
            step(dve.tensor_tensor(flat, flat, factors.rearrange("p t (b o) -> p (t b) o", o=1)
                                   .broadcast_to([P, 2 * tiles, width + 1]), ALU.mult))
            step(dve.tensor_tensor(mixed[:, :, :], sides[:, :, 0, :], sides[:, :, 1, :], ALU.add))
            none = inverse[:, 0, :].rearrange("p (t o) -> p t o", o=1)
            inv = inverse[:, 1, :].rearrange("p (t o) -> p t o", o=1)
            total = mixed[:, :, width:width + 1]
            step(dve.tensor_scalar(none, total, 0.0, None, ALU.is_equal))
            step(dve.tensor_tensor(inv, total, none, ALU.add))
            step(dve.tensor_tensor(empty[:, :, :], none.broadcast_to([P, tiles, width]),
                                   mean.rearrange("p (o k) -> p o k", o=1).broadcast_to([P, tiles, width]), ALU.mult))
            dve.tensor_tensor(mixed[:, :, 0:width], mixed[:, :, 0:width], empty[:, :, :], ALU.add)
            step(dve.reciprocal(inv, inv))
            step(dve.tensor_tensor(out, mixed[:, :, 0:width], inv.broadcast_to([P, tiles, width]), ALU.mult))
            assert step.count == WEIGH

        def general_attention(layer, heads, width, flag_ap, d_rows_dram, s_of, values_in, summed, finish):
            local = ExitStack()
            with local:
                v = values_in
                if v is None:
                    v = sb(f"g_values{layer}", [P, T, F], F32, local)
                d_rows = sb(f"d_rows{layer}", [P, heads, N], F32, local)
                adj_tile = sb(f"adj_tile{layer}", [P, N], I32, local)
                keep = sb(f"keep{layer}", [P, N], F32, local)
                away = sb(f"away{layer}", [P, N], F32, local)
                e = sb(f"e{layer}", [P, N], F32, local)
                eT = sb(f"eT{layer}", [P, 2, BANK], F32, local)
                rowwise = sb(f"rowwise{layer}", [P, 4], F32, local)
                loaded, adj_in, adj_used, chain = sems(*(f"g_{n}{layer}" for n in ("loaded", "adj_in", "adj_used", "chain")))
                masked, expd, turned, turned_out, sums, normed, given = sems(
                    *(f"g_{n}{layer}" for n in ("masked", "expd", "turned", "turned_out", "sums", "normed", "given")))
                B = N // BANK
                with nc.Block() as block:
                    @block.sync
                    def _(sp):
                        with sp.If(sp.value_load(flag_ap, min_val=0, max_val=1) > 0):
                            sp.dma_start(d_rows[:, :, :], d_rows_dram.rearrange("(o h) n -> o h n", o=1)
                                         .broadcast_to([P, heads, N])).then_inc(loaded, 16)
                            if values_in is None:
                                sp.dma_start(v[:, :, :], values_kept).then_inc(loaded, 16)
                            with sp.Fori(0, T) as it:
                                sp.wait_ge(adj_used, it + 1)
                                sp.dma_start(adj_tile[:, :], adj[bass.ds(it * P, P), :]).then_inc(adj_in, 16)

                    @block.vector
                    def _(dve):
                        with dve.If(dve.value_load(flag_ap, min_val=0, max_val=1) > 0):
                            dve.memset(rowwise[:, 3:4], 0.0).then_inc(adj_used, 1)
                            dve.wait_ge(loaded, 16 if values_in is not None else 32)
                            with dve.Fori(0, T) as it:
                                dve.wait_ge(adj_in, it * 16 + 16)
                                dve.tensor_scalar(keep[:, :], adj_tile[:, :], 0.0, None, ALU.is_gt).then_inc(chain, 1)
                                dve.tensor_scalar(away[:, :], adj_tile[:, :], 0.0, -NEG_INF, ALU.is_le, ALU.mult)\
                                    .then_inc(adj_used, 1)
                                for h in range(heads):
                                    q = it * heads + h
                                    c = it * (5 * heads + 1) + 5 * h + 1
                                    dve.wait_ge(chain, c)
                                    dve.tensor_scalar(e[:, :], d_rows[:, h, :], s_of(it, h), None, ALU.add).then_inc(chain, 1)
                                    dve.wait_ge(chain, c + 1)
                                    dve.scalar_tensor_tensor(out=e[:, :], in0=e[:, :], scalar=SLOPE, in1=e[:, :],
                                                             op0=ALU.mult, op1=ALU.max).then_inc(chain, 1)
                                    dve.wait_ge(chain, c + 2)
                                    dve.tensor_tensor(e[:, :], e[:, :], keep[:, :], ALU.mult).then_inc(chain, 1)
                                    dve.wait_ge(chain, c + 3)
                                    dve.wait_ge(adj_used, it + 2)
                                    dve.tensor_tensor(e[:, :], e[:, :], away[:, :], ALU.add).then_inc(chain, 1)
                                    dve.wait_ge(chain, c + 4)
                                    dve.reduce_max(rowwise[:, 0:1], e[:, :], axis=AXX).then_inc(chain, 1)
                                    dve.wait_ge(chain, c + 5)
                                    dve.tensor_scalar(rowwise[:, 1:2], rowwise[:, 0:1], -1.0, None, ALU.mult)\
                                        .then_inc(masked, 1)
                                    dve.wait_ge(expd, q + 1)
                                    dve.reciprocal(rowwise[:, 3:4], rowwise[:, 2:3]).then_inc(normed, 1)
                                    for n in range(B):
                                        dve.wait_ge(turned, q * B + (n + 1))
                                        dve.tensor_copy(eT[:, n % 2, :], bank[n % 2][:, :]).then_inc(turned_out, 1)
                                    dve.wait_ge(sums, q + 1)
                                    dve.wait_ge(normed, q + 1)
                                    dve.tensor_scalar(one(summed[:, bass.ds(it, 1), h * width:(h + 1) * width]),
                                                      bank[2][:, 0:width], rowwise[:, 3:4], None, ALU.mult)\
                                        .then_inc(given, 1)
                            dve.wait_ge(given, T * heads)
                            finish(dve, None)

                    @block.scalar
                    def _(act):
                        with act.If(act.value_load(flag_ap, min_val=0, max_val=1) > 0):
                            with act.Fori(0, T) as it:
                                for h in range(heads):
                                    act.wait_ge(masked, it * heads + (h + 1))
                                    act.activation(e[:, :], e[:, :], ACT.Exp, bias=rowwise[:, 1:2],
                                                   accum_out=rowwise[:, 2:3]).then_inc(expd, 1)
                            finish(None, act)

                    @block.tensor
                    def _(pe):
                        with pe.If(pe.value_load(flag_ap, min_val=0, max_val=1) > 0):
                            pe.wait_ge(loaded, 16 if values_in is not None else 32)
                            with pe.Fori(0, T) as it:
                                for h in range(heads):
                                    q = it * heads + h
                                    pe.wait_ge(expd, q + 1)

                                    def turn(n):
                                        for k in range(4):
                                            j = 4 * n + k
                                            last = pe.transpose(bank[n % 2][:, k * P:(k + 1) * P],
                                                                e[:, j * P:(j + 1) * P], ident[:, :])
                                        last.then_inc(turned, 1)

                                    turn(0)
                                    for n in range(B):
                                        if n + 1 < B:
                                            if n >= 1:
                                                pe.wait_ge(turned_out, q * B + n)
                                            turn(n + 1)
                                        pe.wait_ge(turned_out, q * B + (n + 1))
                                        for k in range(4):
                                            j = 4 * n + k
                                            last = pe.matmul(bank[2][:, 0:width], eT[:, n % 2, k * P:(k + 1) * P],
                                                             v[:, j, h * width:(h + 1) * width],
                                                             start=(j == 0), stop=(j == T - 1))
                                    last.then_inc(sums, 1)

        elu_asked, elu_given, fin = sems("elu_asked", "elu_given", "fin")
        fast0 = ExitStack()
        moving = sb("moving", [P, T, H, W0], BF16, fast0)
        masks = sb("masks", [P, T * C], FP8, fast0)
        raw_masks = sb("raw_masks", [P, T * C], FP8, fast0)
        ring = sb("ring", [P, SLOTS, 2, JU * C], FP8, fast0)
        adj_tiles = sb("adj_tiles", [P, 2, N], BF16, fast0)
        s_rows = sb("s_rows", [P, 2, C], F32, fast0)
        ident_b = sb("ident_b", [P, P], BF16, fast0)
        neg_d = sb("neg_d", [P, H, T], F32, fast0)
        evac = sb("evac", [P, CT, 2, K0], F32, fast0)
        mixed = sb("mixed", [P, CT, K0], F32, fast0)
        empty = sb("empty", [P, CT, D], F32, fast0)
        attended = sb("attended", [P, CT, F], F32, fast0)
        inverse = sb("inverse", [P, 2, CT], F32, fast0)
        low0 = sb("low0", [P, H], F32, fast0)
        centre0 = sb("centre0", [P, H], F32, fast0)
        above_d, below_d = (sb(n, [P, H, T], F32, fast0) for n in ("above_d", "below_d"))

        idle = masks[:, :].bitcast(F32)
        featT = idle[:, 0:N]
        values = idle[:, N:2 * N].rearrange("p (t f) -> p t f", f=F)
        spare = ring[:, :, :, :].rearrange("p s b n -> p (s b n)").bitcast(F32)
        proj = spare[:, 0:F + 2 * H]
        wa = spare[:, 256:256 + 2 * F].rearrange("p (k h d) -> p k h d", k=2, h=H)
        a_row = spare[0:1, 512:512 + 2 * F]
        a1_row = spare[0:1, 768:768 + 2 * F]
        ones = spare[:, 1024:1024 + P]
        seen = spare[:, 1152:1152 + 6 * H + 2]
        column = spare[:, 1200:1201]
        seen_pairs = spare[:, 1208:1208 + T].rearrange("p (k n) -> p k n", k=2)
        turned_scores = spare[0:T, 1280:1280 + 2 * H * P].rearrange("t (k p) -> t k p", k=2 * H)
        parts_b = [spare[:, lo:lo + T * K0].rearrange("p (t k) -> p t k", k=K0) for lo in (2560, 5120)]
        part_d = spare[:, 3840:3840 + T * K0].rearrange("p (t k) -> p t k", k=K0)
        all_columns = moving[:, :, :, :].rearrange("p t h (b q k) -> p t h b q k", b=2, q=PARTS)

        x_in, small_in, ident_zero, ident_ready, ones_ready, ident_b_ready = sems(
            "x_in", "small_in", "ident_zero", "ident_ready", "ones_ready", "ident_b_ready")
        a_spread, dve0, pool0, proj_ready, transposed, T_copied, projected, taken = sems(
            "a_spread", "dve0", "pool0", "proj_ready", "transposed", "T_copied", "projected", "taken")
        extrema_ready, extrema_turned, extrema_given, scores_turned, scores_copied = sems(
            "extrema_ready", "extrema_turned", "extrema_given", "scores_turned", "scores_copied")
        mean_ready, exp_asked, exp_given, scores_out, values_out = sems(
            "mean_ready", "exp_asked", "exp_given", "scores_out", "values_out")
        adj_in = sems("adj_in0", "adj_in1")
        a1_taken, turned, turned_out, mask_ready, kept, pool_done = sems(
            "a1_taken", "turned", "turned_out", "mask_ready", "kept", "pool_done")
        s_in = sems("s_head_in0", "s_head_in1")
        s_read_act, s_read_dve = sems("s_read_act", "s_read_dve")
        signs_ready, compared, below_ready, unit_ready, unit_done, acc_ready, acc_taken = sems(
            "signs_ready", "compared", "below_ready", "unit_ready", "unit_done", "acc_ready", "acc_taken")

        pair_seen, cast_asked, cast_given, side_done = sems("pair_seen", "cast_asked", "cast_given", "side_done")
        turn_bank = [bank[4 + i] for i in range(4)]

        def load_adj(pool, b, t):
            pool.dma_start(adj_tiles[:, t % 2, :], adj[bass.ds(b * C + t * P, P), :]).then_inc(adj_in[t % 2], 16)

        def turn_group(pe, b, q):
            t = q // QT
            if q % QT == 0:
                pe.wait_ge(adj_in[t % 2], b * (8 * CT) + 16 * (t // 2 + 1))
            if isinstance(b, int) and b == 0 and q < 4:
                pass
            else:
                hold(pe, turned_out, b * Q + (q - 3))
            dst = turn_bank[q % 4][:, :].bitcast(BF16)
            for k in range(GQ):
                j = (q % QT) * GQ + k
                last = pe.transpose(dst[:, k * P:(k + 1) * P], adj_tiles[:, t % 2, j * P:(j + 1) * P], ident_b[:, :])
            last.then_inc(turned, 1)

        def take_group(act, b, q):
            t, j = q // QT, (q % QT) * GQ
            hold(act, turned, b * Q + (q + 1))
            dst = raw_masks[:, :].rearrange("p (j i) -> p j i", i=C)
            act.activation(dst[:, j:j + GQ, t * P:(t + 1) * P],
                           turn_bank[q % 4][:, :].bitcast(BF16).rearrange("p (j i) -> p j i", i=P),
                           ACT.Relu, scale=2.0, saturate=False).then_inc(turned_out, 1)

        def two_tiles(n):
            return bank[2 + n % 2][:, 0:2 * (F + 2 * H)].rearrange("p (t k) -> p t k", t=2)

        def groups_of(n):
            return range(EARLY + n, EARLY + n + 1)

        def weigh_values(step, part, h, b, weight):
            weight = weight[:, h, :].rearrange("p (t o) -> p t o", o=1)
            step(step.engine.tensor_tensor(part[:, :, 0:D], values[:, :, h * D:(h + 1) * D],
                                           weight.broadcast_to([P, T, D]), ALU.mult))
            step(step.engine.tensor_copy(part[:, :, D:K0], weight))
            split(step, part, *(all_columns[:, :, h, b, q, :] for q in range(PARTS)))

        sides0 = [(h, 0) for h in range(H)] + [(h, 1) for h in range(H - ON_POOL)]
        side_pairs = [range(i, min(i + 2, len(sides0))) for i in range(0, len(sides0), 2)]

        def side_part(i, q):
            h, b = sides0[i]
            return all_columns[:, :, h, b, q, :]

        def prepare_sides(dve):
            for pair in side_pairs:
                casts = 2 * pair[0]
                for i in pair:
                    h, b = sides0[i]
                    if i == H:
                        dve.wait_ge(exp_given, 2)
                    if i >= 2:
                        dve.wait_ge(side_done, i - 1)
                    part = parts_b[i % 2]
                    weight = (above_d, below_d)[b][:, h, :].rearrange("p (t o) -> p t o", o=1)
                    dve.tensor_tensor(part[:, :, 0:D], values[:, :, h * D:(h + 1) * D],
                                      weight.broadcast_to([P, T, D]), ALU.mult)
                    dve.tensor_copy(part[:, :, D:K0], weight).then_inc(cast_asked, 1)
                for i in pair:
                    dve.wait_ge(cast_given, casts + (i - pair[0]) + 1)
                    dve.tensor_tensor(parts_b[i % 2], parts_b[i % 2], side_part(i, 0), ALU.subtract)\
                        .then_inc(cast_asked, 1)
                for i in pair:
                    dve.wait_ge(cast_given, casts + len(pair) + (i - pair[0]) + 1)
                    dve.tensor_tensor(side_part(i, 2), parts_b[i % 2], side_part(i, 1), ALU.subtract)\
                        .then_inc(side_done, 1)
            dve.wait_ge(side_done, len(sides0))

        def round_sides(act):
            left = list(range(EARLY + T // 2, Q))
            for pair in side_pairs:
                casts = 2 * pair[0]
                for q in range(2):
                    for i in pair:
                        act.wait_ge(cast_asked, casts + q * len(pair) + (i - pair[0]) + 1)
                        act.activation(side_part(i, q), parts_b[i % 2], ACT.Copy).then_inc(cast_given, 1)
                for _ in range(ACT_GROUPS):
                    if left:
                        take_group(act, 0, left.pop(0))
            for q in left:
                take_group(act, 0, q)

        def clean_masks(dve, b, g):
            if g == 0:
                dve.wait_ge(turned_out, b * Q + Q)
            here = slice(g * (JU * C // 4), (g + 1) * (JU * C // 4))
            dve.tensor_scalar(masks[:, :].bitcast(I32)[:, here], raw_masks[:, :].bitcast(I32)[:, here], TWOS, SIGNS,
                              ALU.bitwise_and, ALU.bitwise_or).then_inc(mask_ready, 1)

        with nc.Block() as block:
            @block.sync
            def _(sp):
                sp.dma_start(proj[:, 0:F], W).then_inc(small_in, 16)
                sp.dma_start(a_row, a0.rearrange("o h e -> o (h e)")).then_inc(small_in, 16)
                sp.dma_start(a1_row, a1.rearrange("f o -> o f")).then_inc(small_in, 16)
                sp.dma_start(feat[:, :, :], x_rows).then_inc(x_in, 16)
                sp.wait_ge(taken, T // 2)
                sp.dma_start(values_kept, values).then_inc(values_out, 16)
                sp.wait_ge(scores_copied, 1)
                sp.dma_start(score_rows.rearrange("k (t p) -> t k p", p=P), turned_scores).then_inc(scores_out, 16)
                sp.wait_ge(scores_out, 16)
                for h in range(2):
                    sp.dma_start(s_rows[:, h, :], score_rows[H + h:H + h + 1, 0:C].broadcast_to([P, C]))\
                        .then_inc(s_in[h], 16)
                sp.wait_ge(values_out, 16)
                for h in range(2):
                    sp.wait_ge(s_in[h], 16)

            @block.gpsimd
            def _(pool):
                pool.memset(ones, 1.0).then_inc(ones_ready, 1)
                pool.memset(ident[:, :], 0.0).then_inc(ident_zero, 1)
                pool.wait_ge(ident_zero, 1)
                pool.affine_select(out=ident[:, :], in_=ident[:, :], compare_op=ALU.not_equal, fill=1.0, base=0,
                                   pattern=[[-1, P]], channel_multiplier=1).then_inc(ident_ready, 1)
                load_adj(pool, 0, 0)
                load_adj(pool, 0, 1)
                pool.wait_ge(ident_ready, 1)
                pool.tensor_copy(ident_b[:, :], ident[:, :]).then_inc(ident_b_ready, 1)
                for t in range(2, CT):
                    pool.wait_ge(turned, (t - 1) * QT)
                    load_adj(pool, 0, t)
                step = Chain(pool, pool0)
                pool.wait_ge(exp_given, 2)
                for h in range(H - ON_POOL, H):
                    weigh_values(step, part_d, h, 1, below_d)
                pool.sem_inc(pool_done, 1)

            @block.tensor
            def _(pe):
                pe.wait_ge(small_in, 48)
                pe.wait_ge(ones_ready, 1)
                pe.matmul(bank[2][:, 0:2 * F], ones[0:1, :], a_row, start=True, stop=True)
                pe.matmul(bank[3][:, 0:2 * F], ones[0:1, :], a1_row, start=True, stop=True).then_inc(a_spread, 1)
                pe.wait_ge(ident_b_ready, 1)
                for q in range(EARLY):
                    turn_group(pe, 0, q)
                pe.wait_ge(x_in, 16)
                pe.wait_ge(ident_ready, 1)
                for n in range(T // 4):
                    if n >= 2:
                        pe.wait_ge(T_copied, n - 1)
                    for t in range(4 * n, 4 * n + 4):
                        last = pe.transpose(bank[n % 2][:, (t % 4) * P:(t % 4 + 1) * P], feat[:, t, :], ident[:, :])
                    last.then_inc(transposed, 1)
                pe.wait_ge(proj_ready, 1)
                pe.wait_ge(a1_taken, 1)
                for n in range(T // 2):
                    if n % 2 == 0:
                        pe.wait_ge(T_copied, n // 2 + 1)
                    if n >= 2:
                        pe.wait_ge(taken, n - 1)
                    for t in range(2 * n, 2 * n + 2):
                        at = (t % 2) * (F + 2 * H)
                        last = pe.matmul(bank[2 + n % 2][:, at:at + F + 2 * H], featT[:, t * P:(t + 1) * P], proj,
                                         start=True, stop=True)
                    last.then_inc(projected, 1)
                    for q in groups_of(n):
                        turn_group(pe, 0, q)
                pe.wait_ge(taken, T // 2)
                for k in range(2 * H):
                    last = pe.transpose(bank[k // 4][0:T, (k % 4) * P:(k % 4 + 1) * P], scores[:, :, k], ident[:, :])
                last.then_inc(scores_turned, 1)
                pe.wait_ge(extrema_ready, 1)
                pe.transpose(bank[3][0:4 * H + 2, 0:P], seen[:, 0:4 * H + 2], ident[:, :]).then_inc(extrema_turned, 1)
                pe.wait_ge(extrema_given, 1)
                pe.matmul(bank[3][:, P:P + 4 * H + 2], ones[0:4 * H + 2, :], seen[0:4 * H + 2, 0:4 * H + 2],
                          start=True, stop=True).then_inc(extrema_turned, 1)
                for t in range(T):
                    last = pe.matmul(bank[2][:, 0:F], ones, values[:, t, :], start=(t == 0), stop=(t == T - 1))
                last.then_inc(mean_ready, 1)
                for q in range(EARLY + T // 2, Q):
                    turn_group(pe, 0, q)

            @block.scalar
            def _(act):
                for q in range(EARLY):
                    take_group(act, 0, q)
                for n in range(T // 4):
                    act.wait_ge(transposed, n + 1)
                    act.activation(featT[:, n * BANK:(n + 1) * BANK], bank[n % 2][:, :], ACT.Copy)\
                        .then_inc(T_copied, 1)
                for n in range(T // 2):
                    for q in groups_of(n):
                        take_group(act, 0, q)
                act.wait_ge(scores_turned, 1)
                for k in range(2):
                    last = act.activation(turned_scores[:, 4 * k:4 * k + 4, :].rearrange("t k p -> t (k p)"),
                                          bank[k][0:T, :], ACT.Copy)
                last.then_inc(scores_copied, 1)
                act.wait_ge(exp_asked, 1)
                act.activation(above_d[:, :, :], above_d[:, :, :], ACT.Exp).then_inc(exp_given, 1)
                act.activation(below_d[:, :, :], below_d[:, :, :], ACT.Exp).then_inc(exp_given, 1)
                act.activation(factors[:, :, :, :], factors[:, :, :, :], ACT.Exp).then_inc(exp_given, 1)
                round_sides(act)

            @block.vector
            def _(dve):
                step = Chain(dve, dve0)
                dve.wait_ge(a_spread, 1)
                w_heads = proj[:, 0:F].rearrange("p (h d) -> p h d", h=H)
                a_heads = bank[2][:, 0:2 * F].rearrange("p (h k d) -> p h k d", h=H, k=2)
                for k in range(2):
                    step(dve.tensor_tensor(wa[:, k, :, :], w_heads, a_heads[:, :, k, :], ALU.mult))
                step(dve.reduce_sum(proj[:, F:F + H], wa[:, 1, :, :], axis=AXX))
                dve.reduce_sum(proj[:, F + H:F + 2 * H], wa[:, 0, :, :], axis=AXX).then_inc(proj_ready, 1)
                dve.tensor_copy(a1_spread[:, :, :].rearrange("p k f -> p (k f)"), bank[3][:, 0:2 * F])\
                    .then_inc(a1_taken, 1)

                def extrema_of(n):
                    dve.wait_ge(taken, n + 1)
                    pair = values[:, 2 * n:2 * n + 2, :].rearrange("p t f -> p (t f)")
                    dve.tensor_reduce(seen_pairs[:, 0, n:n + 1], pair, axis=AXX, op=ALU.max)
                    dve.tensor_reduce(seen_pairs[:, 1, n:n + 1], pair, axis=AXX, op=ALU.min).then_inc(pair_seen, 1)

                for n in range(T // 2):
                    dve.wait_ge(projected, n + 1)
                    dve.tensor_copy(values[:, 2 * n:2 * n + 2, :], two_tiles(n)[:, :, 0:F])
                    dve.tensor_copy(scores[:, 2 * n:2 * n + 2, :], two_tiles(n)[:, :, F:F + 2 * H]).then_inc(taken, 1)
                    if n >= 1:
                        extrema_of(n - 1)
                extrema_of(T // 2 - 1)
                by_kind = scores[:, :, :].rearrange("p t k -> p k t")
                dve.tensor_reduce(seen[:, 0:2 * H], by_kind, axis=AXX, op=ALU.max)
                dve.tensor_reduce(seen[:, 2 * H:4 * H], by_kind, axis=AXX, op=ALU.min)
                dve.wait_ge(pair_seen, T // 2)
                dve.tensor_reduce(seen[:, 4 * H:4 * H + 1], seen_pairs[:, 0, :], axis=AXX, op=ALU.max)
                step(dve.tensor_reduce(seen[:, 4 * H + 1:4 * H + 2], seen_pairs[:, 1, :], axis=AXX, op=ALU.min))
                step(dve.tensor_scalar(seen[:, 2 * H:4 * H], seen[:, 2 * H:4 * H], -1.0, None, ALU.mult))
                dve.tensor_scalar(seen[:, 4 * H + 1:4 * H + 2], seen[:, 4 * H + 1:4 * H + 2], -1.0, None, ALU.mult)\
                    .then_inc(extrema_ready, 1)
                bounds(step, H, seen, column, bank[3], low0[:, :], centre0[:, :], flag, extrema_turned, extrema_given)
                exponents(step, exp_asked, H, lambda h: scores[:, :, h], lambda h: scores[:, :, H + h],
                          centre0[:, :], above_d, below_d, factors, neg_d)
                dve.wait_ge(exp_given, 1)
                prepare_sides(dve)
                dve.wait_ge(mean_ready, 1)
                step(dve.tensor_scalar(mean_values[:, :], bank[2][:, 0:F], 1.0 / N, None, ALU.mult))
                dve.wait_ge(exp_given, 3)
                dve.tensor_scalar(factors[:, :, :, 0], factors[:, :, :, 0], -1.0, None, ALU.mult)
                dve.wait_ge(pool_done, 1)
                dve.wait_ge(values_out, 16)
                for g in range(UH):
                    clean_masks(dve, 0, g)


        def finish_ask(dve, source, asked):
            dve.tensor_scalar(work[:, :, :], source, 0.0, None, ALU.min).then_inc(asked, 1)

        def elu_exp(act, c):
            hold(act, elu_asked, c + 1)
            act.activation(work[:, :, :], work[:, :, :], ACT.Exp).then_inc(elu_given, 1)

        FIN = 9

        PIECES = 6

        def close_rows(dve, source, c, given_count, base, piece):
            rows = bass.ds(c * CT, CT) if not isinstance(c, int) else slice(c * CT, (c + 1) * CT)
            flat = lambda ap: ap.rearrange("p t f -> p (t f)")
            if piece == 0:
                dve.wait_ge(elu_given, given_count)
                dve.scalar_tensor_tensor(out=flat(work[:, :, :]), in0=flat(source), scalar=0.0, in1=flat(work[:, :, :]),
                                         op0=ALU.max, op1=ALU.add).then_inc(fin, 1)
            elif piece == 1:
                dve.wait_ge(fin, base + 1)
                dve.scalar_tensor_tensor(out=flat(work[:, :, :]), in0=flat(work[:, :, :]), scalar=-1.0,
                                         in1=flat(feat[:, rows, :]), op0=ALU.add, op1=ALU.add).then_inc(fin, 1)
            elif piece == 2:
                dve.wait_ge(fin, base + 2)
                for t in range(CT):
                    last = dve.bn_stats(stats[:, t, 0:6], work[:, t, :])
                last.then_inc(fin, 1)
            elif piece == 3:
                hold(dve, fin, base + 3)
                for t in range(CT):
                    last = dve.bn_aggr(mean_var[:, t, :], stats[:, t, 0:6])
                last.then_inc(fin, 1)
                dve.wait_ge(fin, base + 4)
                dve.tensor_copy(var[:, rows], mean_var[:, :, 1])
                dve.tensor_tensor(feat[:, rows, :], work[:, :, :], mean_var[:, :, 0:1].broadcast_to([P, CT, F]),
                                  ALU.subtract).then_inc(fin, 1)
            else:
                k = piece - 4
                a = a1_spread[:, k:k + 1, :].broadcast_to([P, CT, F])
                dve.wait_ge(fin, base + 5 + 2 * k)
                dve.tensor_tensor(work[:, :, :], feat[:, rows, :], a, ALU.mult).then_inc(fin, 1)
                dve.wait_ge(fin, base + 6 + 2 * k)
                dve.reduce_sum(dots[:, k, rows], work[:, :, :], axis=AXX).then_inc(fin, 1)

        def slot_halves(u):
            s = u % SLOTS
            return ring[:, s, 0, :], ring[:, s, 1, :]

        def act_count(u):
            return sum(ON_ACT[:u])

        def direct_count(u):
            return sum(DIRECT[:u])

        def wait_s(engine, c, u):
            h = u // UH
            hold(engine, s_in[h % 2], c * 32 + 16 * (h // 2 + 1))

        def act_unit(act, c, u):
            h, g = divmod(u, UH)
            if g == 0:
                wait_s(act, c, u)
            if not ON_ACT[u]:
                return
            hold(act, unit_done, c * U + (u + 1))
            below = slot_halves(u)[1]
            for k in range(JU):
                j = g * JU + k
                last = act.activation(below[:, k * C:(k + 1) * C], s_rows[:, h % 2, :], ACT.Sign,
                                      bias=scores[:, j, h:h + 1], saturate=False)
                if k == JU - 1:
                    last.then_inc(signs_ready, 1)
            if g == UH - 1:
                act.wait_ge(signs_ready, c * NA + act_count(u + 1))
                act.sem_inc(s_read_act, 1)

        def dve_compare(dve, c, u):
            h, g = divmod(u, UH)
            hold(dve, unit_done, c * U + (u + 1))
            below = slot_halves(u)[1].bitcast(U8)
            for k in range(JU):
                j = g * JU + k
                last = dve.tensor_scalar(below[:, k * C:(k + 1) * C], s_rows[:, h % 2, :], neg_d[:, h, j:j + 1],
                                         float(TWO), ALU.is_lt, ALU.mult)
            last.then_inc(compared, 1)

        def dve_unit(dve, c, u, clean=False):
            h, g = divmod(u, UH)
            if g == 0:
                wait_s(dve, c, u)
            if clean and g + 1 < UH:
                clean_masks(dve, c, g + 1)
            if g + 1 < UH and not ON_ACT[u + 1]:
                dve_compare(dve, c, u + 1)
            above, below = (half.bitcast(I32) for half in slot_halves(u))
            m = masks[:, :].bitcast(I32)[:, g * (JU * C // 4):(g + 1) * (JU * C // 4)]
            done = unit_ready if DIRECT[u] else below_ready
            if clean:
                dve.wait_ge(mask_ready, c * UH + (g + 1))
            if ON_ACT[u]:
                dve.wait_ge(signs_ready, c * NA + act_count(u + 1))
                dve.scalar_tensor_tensor(out=below, in0=below, scalar=1, in1=m, op0=ALU.logical_shift_right,
                                         op1=ALU.bitwise_and).then_inc(done, 1)
            else:
                dve.wait_ge(compared, c * ND + (u + 1 - act_count(u + 1)))
                dve.tensor_tensor(below, below, m, ALU.bitwise_and).then_inc(done, 1)
                if all(ON_ACT[u + 1:(h + 1) * UH]):
                    dve.sem_inc(s_read_dve, 1)
            if not DIRECT[u]:
                dve.wait_ge(below_ready, c * (U - sum(DIRECT)) + (u + 1 - direct_count(u + 1)))
                dve.tensor_tensor(above, m, below, ALU.bitwise_xor).then_inc(unit_ready, 1)

        ev_done = sem("ev_done")

        def take_head(dve, c, h):
            for b in range(CT // 2):
                dve.wait_ge(acc_ready, c * (H * NB) + (h * NB + b + 1))
                parts = bank[b][:, 0:2 * W0].rearrange("p (m q k) -> p m k q", q=PARTS, k=K0)
                dve.tensor_reduce(evac[:, 2 * b:2 * b + 2, :, :].rearrange("p t b k -> p (t b) k"), parts, axis=AXX,
                                  op=ALU.add).then_inc(acc_taken, 1)
            dve.wait_ge(acc_taken, c * (H * NB) + ((h + 1) * NB + NB))
            rows = bass.ds(c * CT, CT) if not isinstance(c, int) else slice(c * CT, (c + 1) * CT)
            weigh(dve, ev_done, c * (WEIGH * H) + WEIGH * h, evac, mixed, empty, inverse, factors[:, h, rows, :],
                  mean_values[:, h * D:(h + 1) * D], D, CT, attended[:, :, h * D:(h + 1) * D])

        def pe_chunk(pe, c, build):
            for u in range(U):
                h, g = divmod(u, UH)
                if build:
                    for q in groups_at(u):
                        turn_group(pe, c + 1, q)
                hold(pe, unit_ready, c * U + (u + 1))
                above, below = slot_halves(u)
                for t in range(CT):
                    b, at = t // 2, (t % 2) * W0
                    if g == 0 and t % 2 == 0:
                        hold(pe, acc_taken, c * (H * NB) + (h * NB + b + 1))
                    for k in range(JU):
                        j = g * JU + k
                        mine = slice(k * C + t * P, k * C + (t + 1) * P)
                        if DIRECT[u]:
                            of_all = masks[:, j * C + t * P:j * C + (t + 1) * P]
                            weighed = ((of_all, 0, PARTS * K0), (below[:, mine], 0, W0))
                        else:
                            weighed = ((above[:, mine], 0, PARTS * K0), (below[:, mine], PARTS * K0, W0))
                        for mask, lo, hi in weighed:
                            first = j == 0 and t % 2 == 0 and mask is weighed[0][0]
                            last = pe.matmul(bank[b][:, at + lo:at + hi], mask, moving[:, j, h, lo:hi],
                                             start=first, stop=(j == T - 1), skip_group_check=True)
                    if g == UH - 1 and t % 2 == 1:
                        last.then_inc(acc_ready, 1)
                    elif t == CT - 1:
                        last.then_inc(unit_done, 1)
                if g == UH - 1:
                    pe.wait_ge(acc_ready, c * (H * NB) + (h + 1) * NB)
                    pe.sem_inc(unit_done, 1)

        def only_if(engine, flag_ap, wanted):
            value = engine.value_load(flag_ap, min_val=0, max_val=1)
            return engine.If(value > 0 if wanted else value < 1)

        with nc.Block() as block:
            @block.gpsimd
            def _(pool):
                with only_if(pool, flag[0:1, 0:1], False):
                    with pool.Fori(0, NC - 1) as c:
                        for t in range(CT):
                            pool.wait_ge(turned, c * Q + (Q + (t - 1) * QT))
                            load_adj(pool, c + 1, t)

            @block.sync
            def _(sp):
                with only_if(sp, flag[0:1, 0:1], False):
                    def keep(c):
                        sp.wait_ge(mask_ready, c * UH + UH)
                        dst = masks_kept[bass.ds(c, 1), :, :, :] if not isinstance(c, int) else masks_kept[c:c + 1, :, :, :]
                        sp.dma_start(dst.rearrange("o p t i -> (o p) (t i)"), masks[:, :].bitcast(I32)).then_inc(kept, 16)

                    def load_s(c, h, before):
                        sp.wait_ge(s_read_act, before)
                        sp.wait_ge(s_read_dve, before)
                        cols = bass.ds(c * C, C) if not isinstance(c, int) else slice(c * C, (c + 1) * C)
                        sp.dma_start(s_rows[:, h % 2, :], score_rows[H + h:H + h + 1, cols].broadcast_to([P, C]))\
                            .then_inc(s_in[h % 2], 16)

                    with sp.Fori(0, NC - 1) as c:
                        keep(c)
                        load_s(c, 2, c * H + 1)
                        load_s(c, 3, c * H + 2)
                        load_s(c + 1, 0, c * H + 3)
                        load_s(c + 1, 1, c * H + 4)
                    keep(NC - 1)
                    load_s(NC - 1, 2, (NC - 1) * H + 1)
                    load_s(NC - 1, 3, (NC - 1) * H + 2)
                    sp.wait_ge(kept, 16 * NC)

            @block.tensor
            def _(pe):
                with only_if(pe, flag[0:1, 0:1], False):
                    pe.sem_inc(unit_done, SLOTS)
                    pe.sem_inc(acc_taken, NB)
                    with pe.Fori(0, NC - 1) as c:
                        pe_chunk(pe, c, True)
                    pe_chunk(pe, NC - 1, False)

            @block.scalar
            def _(act):
                with only_if(act, flag[0:1, 0:1], False):
                    def part(c, units, build):
                        for u in units:
                            act_unit(act, c, u)
                            if build:
                                for q in groups_at(u - LAG):
                                    if q == 0:
                                        hold(act, mask_ready, c * UH + UH)
                                    take_group(act, c + 1, q)

                    part(0, range(ROT), False)
                    with act.Fori(0, NC - 1) as c:
                        part(c, range(ROT, U), True)
                        part(c + 1, range(5), False)
                        elu_exp(act, c)
                        part(c + 1, range(5, ROT), False)
                    part(NC - 1, range(ROT, U), False)
                    elu_exp(act, NC - 1)

            @block.vector
            def _(dve):
                with only_if(dve, flag[0:1, 0:1], False):
                    def units(c, which, clean=False):
                        for u in which:
                            dve_unit(dve, c, u, clean)
                            for h in range(H - 1):
                                if u == UH * (h + 1) + 1:
                                    take_head(dve, c, h)

                    def close(c):
                        take_head(dve, c, H - 1)
                        dve.wait_ge(ev_done, c * (WEIGH * H) + WEIGH * H)
                        finish_ask(dve, attended[:, :, :], elu_asked)

                    dve.wait_ge(mask_ready, UH)
                    units(0, range(DVE_ROT))
                    with dve.Fori(0, NC - 1) as c:
                        units(c, range(DVE_ROT, U))
                        hold(dve, kept, c * 16 + 16)
                        dve.wait_ge(unit_ready, c * U + U)
                        clean_masks(dve, c + 1, 0)
                        for u in range(DVE_ROT):
                            units(c + 1, (u,), u < UH)
                            if u == CLOSE_AT:
                                close(c)
                            if u in PIECES_AT:
                                close_rows(dve, attended[:, :, :], c, c + 1, c * FIN, PIECES_AT.index(u))
                    units(NC - 1, range(DVE_ROT, U))
                    close(NC - 1)
                    for piece in range(PIECES):
                        close_rows(dve, attended[:, :, :], NC - 1, NC, (NC - 1) * FIN, piece)

        fast0.close()

        general0 = ExitStack()
        summed = sb("summed", [P, T, F], F32, general0)

        def finish0(dve, act):
            for c in range(NC):
                if dve is not None:
                    source = summed[:, c * CT:(c + 1) * CT, :]
                    finish_ask(dve, source, elu_asked)
                    for piece in range(PIECES):
                        close_rows(dve, source, c, c + 1, c * FIN, piece)
                    dve.wait_ge(fin, c * FIN + FIN)
                else:
                    elu_exp(act, c)

        general_attention(0, H, D, flag[0:1, 0:1], score_rows[0:H, :],
                          lambda it, h: one(scores[:, bass.ds(it, 1), H + h:H + h + 1]), None, summed, finish0)
        general0.close()

        moving1 = sb("moving1", [P, T, 2 * PARTS * K1], BF16)
        values1 = sb("values1", [P, T, F])
        scores1 = sb("scores1", [P, T, 2])
        inv_std = sb("inv_std", [P, T])
        rows = sb("rows", [P, 12, T])
        turned_scores1 = sb("turned_scores1", [T, 2, P])
        factors1 = sb("factors1", [P, 1, T, 2])
        above_d1, below_d1, neg_d1 = (sb(n, [P, 1, T]) for n in ("above_d1", "below_d1", "neg_d1"))
        seen1, column1, low1, centre1 = sb("seen1", [P, 8]), sb("column1", [P, 1]), sb("low1", [P, 1]), sb("centre1", [P, 1])
        ones1 = sb("ones1", [P, P])
        mean_values1 = sb("mean_values1", [P, F])
        work1 = sb("work1", [P, RT, F])
        result = sb("result", [P, 2, RT, F])
        small = sb("small", [P, 8, RT])
        stats1 = sb("stats1", [P, RT, 8])
        mean_var1 = sb("mean_var1", [P, RT, 2])
        fast1 = ExitStack()
        pair = sb("pair", [P, 2, 2, T * R], FP8, fast1)
        s_rows1 = sb("s_rows1", [P, 2, R], F32, fast1)
        GT = 8
        NG = T // GT
        part_d1 = sb("part_d1", [P, GT, K1], F32, fast1)
        sides1 = [sb(n, [P, GT, K1], F32, fast1) for n in ("part_above1", "part_below1")]

        roots_asked, roots_given, logs_asked, logs_given, dve1 = sems(
            "roots_asked", "roots_given", "logs_asked", "logs_given", "dve1")
        scores1_ready, scores1_turned, scores1_copied, scores1_out = sems(
            "scores1_ready", "scores1_turned", "scores1_copied", "scores1_out")
        values1_ready, mean1_ready, ones1_ready, exp1_asked, exp1_given = sems(
            "values1_ready", "mean1_ready", "ones1_ready", "exp1_asked", "exp1_given")
        extrema1_ready, extrema1_turned, extrema1_given = sems("extrema1_ready", "extrema1_turned", "extrema1_given")
        mask_in = sems("mask_in0", "mask_in1")
        s_run_in = sems("s_run_in0", "s_run_in1")

        def over(ap, tiles, width):
            return ap.rearrange("p (t o) -> p t o", o=1).broadcast_to([P, tiles, width])

        def load_run(sp, e, y):
            load_masks(sp, e, y)
            load_s(sp, e, y)

        def load_masks(sp, e, y):
            per = C // R
            words = slice((y % per) * R // 4, (y % per + 1) * R // 4)
            src = masks_kept[bass.ds(e // per, 1), :, :, words] if not isinstance(e, int) else \
                masks_kept[e // per:e // per + 1, :, :, words]
            sp.dma_start(pair[:, y, 0, :].bitcast(I32).rearrange("p (t i) -> p t i", i=R // 4),
                         src.rearrange("o p t i -> (o p) t i"))\
                .then_inc(mask_in[y], 16)

        def load_s(sp, e, y):
            cols = slice(e * R, (e + 1) * R) if isinstance(e, int) else bass.ds(e * R, R)
            sp.dma_start(s_rows1[:, y, :], score_rows1[1:2, cols].broadcast_to([P, R])).then_inc(s_run_in[y], 16)

        with nc.Block() as block:
            @block.gpsimd
            def _(pool):
                pool.memset(ones1[:, :], 1.0).then_inc(ones1_ready, 1)

            @block.sync
            def _(sp):
                with only_if(sp, flag[0:1, 0:1], False):
                    load_masks(sp, 0, 0)
                    sp.wait_ge(mask_in[0], 16)
                sp.wait_ge(scores1_copied, 1)
                sp.dma_start(score_rows1.rearrange("k (t p) -> t k p", p=P), turned_scores1[:, :, :]).then_inc(scores1_out, 16)
                sp.wait_ge(scores1_out, 16)
                for y in range(2):
                    load_s(sp, y, y)
                for y in range(2):
                    sp.wait_ge(s_run_in[y], 16)

            @block.scalar
            def _(act):
                act.wait_ge(roots_asked, 1)
                act.activation(rows[:, 2:4, :], rows[:, 0:2, :], ACT.Sqrt).then_inc(roots_given, 1)
                act.wait_ge(logs_asked, 1)
                act.activation(rows[:, 8:10, :], rows[:, 8:10, :], ACT.Ln).then_inc(logs_given, 1)
                act.wait_ge(scores1_turned, 1)
                act.activation(turned_scores1[:, :, :].rearrange("t k p -> t (k p)"), bank[0][0:T, 0:2 * P], ACT.Copy)\
                    .then_inc(scores1_copied, 1)
                act.wait_ge(exp1_asked, 1)
                act.activation(above_d1[:, :, :], above_d1[:, :, :], ACT.Exp).then_inc(exp1_given, 1)
                act.activation(below_d1[:, :, :], below_d1[:, :, :], ACT.Exp).then_inc(exp1_given, 1)
                act.activation(factors1[:, :, :, :], factors1[:, :, :, :], ACT.Exp).then_inc(exp1_given, 1)

            @block.tensor
            def _(pe):
                pe.wait_ge(scores1_ready, 1)
                for k in range(2):
                    last = pe.transpose(bank[0][0:T, k * P:(k + 1) * P], scores1[:, :, k], ident[:, :])
                last.then_inc(scores1_turned, 1)
                pe.wait_ge(ones1_ready, 1)
                pe.wait_ge(extrema1_ready, 1)
                pe.transpose(bank[3][0:6, 0:P], seen1[:, 0:6], ident[:, :]).then_inc(extrema1_turned, 1)
                pe.wait_ge(extrema1_given, 1)
                pe.matmul(bank[3][:, P:P + 6], ones1[0:6, :], seen1[0:6, 0:6], start=True, stop=True)\
                    .then_inc(extrema1_turned, 1)

            @block.vector
            def _(dve):
                step = Chain(dve, dve1)
                step(dve.tensor_scalar(rows[:, 0, :], var[:, :], LN_EPS, None, ALU.add))
                dve.tensor_scalar(rows[:, 1, :], var[:, :], float(F), None, ALU.mult).then_inc(roots_asked, 1)
                dve.wait_ge(roots_given, 1)
                newton_root(step, rows[:, 2:4, :], rows[:, 0:2, :], rows[:, 4:6, :])
                norm, square, scratch, ratio, near = (rows[:, k, :] for k in (6, 7, 10, 11, 5))
                plus, minus = rows[:, 8, :], rows[:, 9, :]
                step(dve.reciprocal(inv_std[:, :], rows[:, 2, :]))
                step(dve.tensor_tensor(norm, rows[:, 3, :], inv_std[:, :], ALU.mult))
                step(dve.tensor_scalar(norm, norm, EPS, 1.0 - EPS, ALU.max, ALU.min))
                dve.tensor_scalar(plus, norm, 1.0, None, ALU.add)
                dve.tensor_scalar(minus, norm, -1.0, 1.0, ALU.mult, ALU.add).then_inc(logs_asked, 1)
                step(dve.reciprocal(scratch, norm))
                step(dve.tensor_tensor(square, norm, norm, ALU.mult))
                step(dve.tensor_scalar(near, square, 1.0 / 9, 1.0 / 7, ALU.mult, ALU.add))
                for c in (5, 3, 1):
                    step(dve.tensor_tensor(near, near, square, ALU.mult))
                    step(dve.tensor_scalar(near, near, 1.0 / c, None, ALU.add))
                step(dve.tensor_scalar(square, norm, 0.1, None, ALU.is_lt))
                dve.wait_ge(logs_given, 1)
                step(dve.tensor_tensor(ratio, plus, minus, ALU.subtract))
                step(dve.tensor_tensor(ratio, ratio, scratch, ALU.mult))
                step(dve.tensor_scalar(ratio, ratio, 0.5, None, ALU.mult))
                step(dve.tensor_tensor(near, near, ratio, ALU.subtract))
                step(dve.tensor_tensor(near, near, square, ALU.mult))
                step(dve.tensor_tensor(ratio, ratio, near, ALU.add))
                step(dve.tensor_tensor(ratio, ratio, inv_std[:, :], ALU.mult))
                dve.tensor_tensor(scores1[:, :, 0], dots[:, 1, :], ratio, ALU.mult)
                dve.tensor_tensor(scores1[:, :, 1], dots[:, 0, :], ratio, ALU.mult).then_inc(scores1_ready, 1)
                dve.wait_ge(scores1_ready, 1)
                by_kind = scores1[:, :, :].rearrange("p t k -> p k t")
                step(dve.memset(seen1[:, :], 0.0))
                dve.tensor_reduce(seen1[:, 0:2], by_kind, axis=AXX, op=ALU.max)
                step(dve.tensor_reduce(seen1[:, 2:4], by_kind, axis=AXX, op=ALU.min))
                dve.tensor_scalar(seen1[:, 2:4], seen1[:, 2:4], -1.0, None, ALU.mult).then_inc(extrema1_ready, 1)
                dve.tensor_tensor(values1[:, :, :], feat[:, :, :], over(ratio, T, F), ALU.mult).then_inc(values1_ready, 1)
                bounds(step, 1, seen1, column1, bank[3], low1[:, :], centre1[:, :], flag1, extrema1_turned, extrema1_given)
                step(dve.tensor_tensor(flag1[0:1, 0:1], flag1[0:1, 0:1], flag[0:1, 0:1], ALU.max))
                exponents(step, exp1_asked, 1, lambda h: scores1[:, :, 0], lambda h: scores1[:, :, 1],
                          centre1[:, :], above_d1, below_d1, factors1, neg_d1)

        evac1 = sb("evac1", [P, RT, 2, K1], F32, fast1)
        mixed1 = sb("mixed1", [P, RT, K1], F32, fast1)
        empty1 = sb("empty1", [P, RT, F], F32, fast1)
        inverse1 = sb("inverse1", [P, 2, RT], F32, fast1)
        attended1 = sb("attended1", [P, RT, F], F32, fast1)
        signs1_ready, compared1, below1_ready, group_ready, tile_ready, pair_taken = sems(
            "signs1_ready", "compared1", "below1_ready", "group_ready", "tile_ready", "pair_taken")
        norm_done, close_done, func_asked, func_given, result_ready = sems(
            "norm_done", "close_done", "func_asked", "func_given", "result_ready")
        stored = sems("stored_even", "stored_odd")
        POOL_GROUPS = 2
        HALF = GT // 2

        def run_rows(e):
            return slice(e * RT, (e + 1) * RT) if isinstance(e, int) else bass.ds(e * RT, RT)

        mean1_taken = sem("mean1_taken")
        dve2, pool1, below_weighed, moving1_ready = sems("dve2", "pool1", "below_weighed", "moving1_ready")

        def weigh_group(step, g, b, part, weight):
            js = slice(g * GT, (g + 1) * GT)
            weight = weight[:, 0, js]
            step(step.engine.tensor_tensor(part[:, :, 0:F], values1[:, js, :], over(weight, GT, F), ALU.mult))
            step(step.engine.tensor_copy(part[:, :, F:K1], weight.rearrange("p (t o) -> p t o", o=1)))
            split(step, part[:, :, :], *(moving1[:, js, (b * PARTS + q) * K1:(b * PARTS + q + 1) * K1]
                                         for q in range(PARTS)))

        def sides_of(g):
            return (0, 1) if g < NG - POOL_GROUPS else (0,)

        def casts_before(g):
            return 2 * sum(len(sides_of(k)) for k in range(g))

        def moving_part(g, b, q):
            return moving1[:, g * GT:(g + 1) * GT, (b * PARTS + q) * K1:(b * PARTS + q + 1) * K1]

        cast1_asked, cast1_given = sems("cast1_asked", "cast1_given")
        CLOSE = 29

        def close_run(dve, v, e, y):
            step = Chain(dve, close_done, e * CLOSE)
            raw2, raw, scratch, norm, gain, big, root = (small[:, k, :] for k in range(7))
            step(dve.tensor_tensor(work1[:, :, :], v, v, ALU.mult))
            step(dve.reduce_sum(raw2, work1[:, :, :], axis=AXX))
            dve.tensor_copy(norm, raw2).then_inc(func_asked, 1)
            dve.wait_ge(func_given, e * 3 + 1)
            newton_root(step, raw, raw2, scratch)
            step(dve.tensor_scalar(norm, raw, EPS, None, ALU.max))
            dve.tensor_copy(scratch, norm).then_inc(func_asked, 1)
            dve.wait_ge(func_given, e * 3 + 2)
            step(dve.reciprocal(scratch, norm))
            step(dve.tensor_tensor(gain, gain, scratch, ALU.mult))
            step(dve.tensor_tensor(norm, gain, raw, ALU.mult))
            step(dve.tensor_scalar(norm, norm, EPS, None, ALU.max))
            step(dve.tensor_scalar(big, norm, MAX_NORM, None, ALU.is_gt))
            step(dve.reciprocal(scratch, norm))
            step(dve.tensor_scalar(scratch, scratch, MAX_NORM, -1.0, ALU.mult, ALU.add))
            step(dve.tensor_tensor(scratch, scratch, big, ALU.mult))
            step(dve.tensor_scalar(scratch, scratch, 1.0, None, ALU.add))
            step(dve.tensor_tensor(gain, gain, scratch, ALU.mult))
            dve.wait_ge(stored[y], (e - y) * 8 + 16)
            step(dve.tensor_tensor(work1[:, :, :], v, over(gain, RT, F), ALU.mult))
            step(dve.tensor_tensor(result[:, y, :, :], feat[:, run_rows(e), :], over(inv_std[:, run_rows(e)], RT, F), ALU.mult))
            step(dve.tensor_tensor(result[:, y, :, :], result[:, y, :, :], work1[:, :, :], ALU.add))
            for t in range(RT):
                last = dve.bn_stats(stats1[:, t, 0:6], result[:, y, t, :])
            step(last)
            if not isinstance(e, int):
                dve.sem_inc(passed, 1)
            for t in range(RT):
                last = dve.bn_aggr(mean_var1[:, t, :], stats1[:, t, 0:6])
            step(last)
            dve.tensor_scalar(raw2, mean_var1[:, :, 1], LN_EPS, None, ALU.add).then_inc(func_asked, 1)
            dve.wait_ge(func_given, e * 3 + 3)
            newton_root(step, root, raw2, scratch)
            step(dve.reciprocal(root, root))
            for t in range(RT):
                last = dve.tensor_scalar(result[:, y, t, :], result[:, y, t, :], mean_var1[:, t, 0:1], root[:, t:t + 1],
                                         ALU.subtract, ALU.mult)
            last.then_inc(result_ready, 1)
            assert step.count == CLOSE, step.count

        def free_results(act):
            for y in range(2):
                act.sem_inc(stored[y], 16)

        def wait_results(act):
            for y in range(2):
                act.wait_ge(stored[y], 16 + 8 * NR)

        def close_act(act, e, y):
            raw2, raw, scratch, norm, gain, big, root = (small[:, k, :] for k in range(7))
            for n, (to, frm, func) in enumerate(((raw, norm, ACT.Sqrt), (gain, scratch, ACT.Tanh), (root, raw2, ACT.Sqrt))):
                act.wait_ge(func_asked, e * 3 + (n + 1))
                act.activation(to, frm, func).then_inc(func_given, 1)
            act.wait_ge(result_ready, e + 1)
            act.dma_start(out_rows[:, run_rows(e), :], result[:, y, :, :]).then_inc(stored[y], 16)

        with nc.Block() as block:
            @block.gpsimd
            def _(pool):
                with only_if(pool, flag1[0:1, 0:1], False):
                    step = Chain(pool, pool1)
                    for g in range(NG - POOL_GROUPS, NG):
                        weigh_group(step, g, 1, part_d1, below_d1)
                        pool.sem_inc(below_weighed, 1)

            @block.sync
            def _(sp):
                with only_if(sp, flag1[0:1, 0:1], False):
                    load_masks(sp, 1, 1)
                    with sp.Fori(0, NR // 2 - 1) as n:
                        for y in range(2):
                            sp.wait_ge(tile_ready, n * (2 * RT) + RT * (y + 1))
                            load_run(sp, n * 2 + (2 + y), y)

            @block.scalar
            def _(act):
                with only_if(act, flag1[0:1, 0:1], False):
                    free_results(act)

                    def round_group(g):
                        sides = sides_of(g)
                        for q in range(2):
                            for b in sides:
                                act.wait_ge(cast1_asked, casts_before(g) + q * len(sides) + b + 1)
                                act.activation(moving_part(g, b, q), sides1[b][:, :, :], ACT.Copy).then_inc(cast1_given, 1)

                    def signs(e, y, round_too=False):
                        hold(act, s_run_in[y], (e - y) * 8 + 16)
                        for g in range(NG):
                            for k in range(HALF):
                                j = g * GT + k
                                last = act.activation(pair[:, y, 1, j * R:(j + 1) * R], s_rows1[:, y, :], ACT.Sign,
                                                      bias=scores1[:, j, 0:1], saturate=False)
                            last.then_inc(signs1_ready, 1)
                            if round_too:
                                round_group(g)

                    signs(0, 0, round_too=True)
                    signs(1, 1)
                    with act.Fori(0, NR // 2 - 1) as n:
                        for y in range(2):
                            close_act(act, n * 2 + y, y)
                            hold(act, tile_ready, n * (2 * RT) + RT * (y + 1))
                            signs(n * 2 + (2 + y), y)
                    for y in range(2):
                        close_act(act, NR - 2 + y, y)
                    wait_results(act)

            @block.tensor
            def _(pe):
                with only_if(pe, flag1[0:1, 0:1], False):
                    pe.sem_inc(pair_taken, RT)
                    for t in range(T):
                        last = pe.matmul(bank[2][:, 0:F], ones1[:, :], values1[:, t, :], start=(t == 0), stop=(t == T - 1))
                    last.then_inc(mean1_ready, 1)

                    def run(e, y):
                        for t in range(RT):
                            hold(pe, pair_taken, e * RT + (t + 1))
                            for j in range(T):
                                if t == 0 and j % GT == 0:
                                    hold(pe, group_ready, e * NG + (j // GT + 1))
                                for side in range(2):
                                    last = pe.matmul(bank[2 * t + side][:, 0:PARTS * K1],
                                                     pair[:, y, side, j * R + t * P:j * R + (t + 1) * P],
                                                     moving1[:, j, side * PARTS * K1:(side + 1) * PARTS * K1],
                                                     start=(j == 0), stop=(j == T - 1))
                            last.then_inc(tile_ready, 1)

                    def first_run():
                        pe.wait_ge(pair_taken, RT)
                        pe.wait_ge(mean1_taken, 1)
                        for j in range(T):
                            if j % GT == 0:
                                pe.wait_ge(group_ready, j // GT + 1)
                                pe.wait_ge(moving1_ready, j // GT + 1)
                                if j // GT >= NG - POOL_GROUPS:
                                    pe.wait_ge(below_weighed, j // GT - (NG - POOL_GROUPS) + 1)
                            for t in range(RT):
                                for side in range(2):
                                    last = pe.matmul(bank[2 * t + side][:, 0:PARTS * K1],
                                                     pair[:, 0, side, j * R + t * P:j * R + (t + 1) * P],
                                                     moving1[:, j, side * PARTS * K1:(side + 1) * PARTS * K1],
                                                     start=(j == 0), stop=(j == T - 1))
                                if j == T - 1:
                                    last.then_inc(tile_ready, 1)

                    first_run()
                    run(1, 1)
                    with pe.Fori(1, NR // 2) as n:
                        for y in range(2):
                            run(n * 2 + y, y)

            @block.vector
            def _(dve):
                with only_if(dve, flag1[0:1, 0:1], False):
                    step = Chain(dve, dve2)

                    def prepare(g):
                        sides, casts = sides_of(g), casts_before(g)
                        for b in sides:
                            weight = (above_d1, below_d1)[b][:, 0, g * GT:(g + 1) * GT]
                            if g > 0:
                                dve.wait_ge(moving1_ready, g)
                            dve.tensor_tensor(sides1[b][:, :, 0:F], values1[:, g * GT:(g + 1) * GT, :],
                                              over(weight, GT, F), ALU.mult)
                            dve.tensor_copy(sides1[b][:, :, F:K1], weight.rearrange("p (t o) -> p t o", o=1))\
                                .then_inc(cast1_asked, 1)
                        for b in sides:
                            dve.wait_ge(cast1_given, casts + b + 1)
                            dve.tensor_tensor(sides1[b][:, :, :], sides1[b][:, :, :], moving_part(g, b, 0), ALU.subtract)\
                                .then_inc(cast1_asked, 1)
                        for b in sides:
                            dve.wait_ge(cast1_given, casts + len(sides) + b + 1)
                            last = dve.tensor_tensor(moving_part(g, b, 2), sides1[b][:, :, :], moving_part(g, b, 1),
                                                     ALU.subtract)
                        last.then_inc(moving1_ready, 1)

                    def split_masks(e, y, weigh_too=False):
                        hold(dve, mask_in[y], (e - y) * 8 + 16)
                        hold(dve, s_run_in[y], (e - y) * 8 + 16)
                        s = s_rows1[:, y, :]
                        above, below = (pair[:, y, k, :] for k in range(2))
                        w = lambda ap, lo, n: ap.bitcast(I32)[:, lo * R // 4:(lo + n) * R // 4]
                        for g in range(NG):
                            for k in range(HALF, GT):
                                j = g * GT + k
                                last = dve.tensor_scalar(below[:, j * R:(j + 1) * R].bitcast(U8), s, neg_d1[:, 0, j:j + 1],
                                                         float(TWO), ALU.is_lt, ALU.mult)
                            last.then_inc(compared1, 1)
                            dve.wait_ge(signs1_ready, e * NG + (g + 1))
                            signs, here = w(below, g * GT, HALF), w(above, g * GT, HALF)
                            dve.scalar_tensor_tensor(out=signs, in0=signs, scalar=1, in1=here,
                                                     op0=ALU.logical_shift_right, op1=ALU.bitwise_and)
                            dve.wait_ge(compared1, e * NG + (g + 1))
                            mine, here = w(below, g * GT + HALF, HALF), w(above, g * GT + HALF, HALF)
                            dve.tensor_tensor(mine, mine, here, ALU.bitwise_and).then_inc(below1_ready, 1)
                            dve.wait_ge(below1_ready, e * NG + (g + 1))
                            dve.tensor_tensor(w(above, g * GT, GT), w(above, g * GT, GT), w(below, g * GT, GT),
                                              ALU.bitwise_xor).then_inc(group_ready, 1)
                            if weigh_too and g + 1 < NG:
                                prepare(g + 1)

                    def take_run(e, y):
                        for t in range(RT):
                            dve.wait_ge(tile_ready, e * RT + (t + 1))
                            for side in range(2):
                                parts = bank[2 * t + side][:, 0:PARTS * K1].rearrange("p (q k) -> p k q", q=PARTS)
                                last = dve.tensor_reduce(evac1[:, t, side, :], parts, axis=AXX, op=ALU.add)
                            last.then_inc(pair_taken, 1)
                        dve.wait_ge(pair_taken, e * RT + 2 * RT)
                        weigh(dve, norm_done, e * WEIGH, evac1, mixed1, empty1, inverse1, factors1[:, 0, run_rows(e), :],
                              mean_values1[:, :], F, RT, attended1[:, :, :])
                        close_run(dve, attended1[:, :, :], e, y)

                    step(dve.tensor_scalar(factors1[:, :, :, 0], factors1[:, :, :, 0], -1.0, None, ALU.mult))
                    prepare(0)
                    dve.wait_ge(mean1_ready, 1)
                    dve.tensor_scalar(mean_values1[:, :], bank[2][:, 0:F], 1.0 / N, None, ALU.mult).then_inc(mean1_taken, 1)
                    split_masks(0, 0, weigh_too=True)
                    split_masks(1, 1)
                    with dve.Fori(0, NR // 2 - 1) as n:
                        for y in range(2):
                            take_run(n * 2 + y, y)
                            split_masks(n * 2 + (2 + y), y)
                    for y in range(2):
                        take_run(NR - 2 + y, y)

        fast1.close()

        def finish1(dve, act):
            if act is not None:
                free_results(act)
            for e in range(NR):
                if dve is not None:
                    close_run(dve, summed1[:, e * RT:(e + 1) * RT, :], e, e % 2)
                else:
                    close_act(act, e, e % 2)
            if act is not None:
                wait_results(act)

        summed1 = sb("summed1", [P, T, F])
        general_attention(1, 1, F, flag1[0:1, 0:1], score_rows1[0:1, :],
                          lambda it, h: one(scores1[:, bass.ds(it, 1), 1:2]), values1, summed1, finish1)


_INS = ['x', 'adj', 'L0_gnn_W', 'L0_gnn_a', 'L1_gnn_a']
_OUTS = [((4096, 128), 'float32')]


def kernel(**inputs):
    import numpy as _np
    import concourse.bacc as _bacc
    from concourse import mybir as _mybir
    from concourse.bass_utils import run_bass_kernel_spmd as _run

    nc = _bacc.Bacc("TRN2", target_bir_lowering=False, num_devices=1)
    arrays, args = {}, []
    for name in _INS:
        a = _np.ascontiguousarray(inputs[name])
        arrays[f"in_{name}_dram"] = a
        args.append(nc.dram_tensor(f"in_{name}_dram", a.shape, _mybir.dt.from_np(a.dtype), kind="ExternalInput").ap())
    for i, (shape, dtype) in enumerate(_OUTS):
        dt = _mybir.dt.from_np(_np.dtype(dtype))
        args.append(nc.dram_tensor(f"out_{i}_dram", shape, dt, kind="ExternalOutput").ap())
    two_layer_gat(nc, *args)
    r = _run(nc, [arrays], core_ids=[0])
    return r.results[0]["out_0_dram"]
```
